# Optimizing a Trainium2 kernel written in Bass

```python
import numpy as np
import jax
import jax.numpy as jnp

def _softmax(x, axis=-1):
    return jax.nn.softmax(x, axis=axis)
def _gelu(x):
    return jax.nn.gelu(x, approximate=True)
def _silu(x):
    return jax.nn.silu(x)
def _sigmoid(x):
    return jax.nn.sigmoid(x)
def _layernorm(x, axis=-1, eps=1e-5):
    m = jnp.mean(x, axis=axis, keepdims=True)
    v = jnp.var(x, axis=axis, keepdims=True)
    return (x - m) / jnp.sqrt(v + eps)
def _scatter_add(tgt, idx, src, axis=0):
    return tgt.at[idx].add(src)
def _segment_sum(src, seg, n):
    return jax.ops.segment_sum(src, seg, n)

kernel_name = 'mk_conv_seq_d2_conv_nchw128_903606'

def setup_inputs(seed: int = 0):
    np.random.seed(seed)
    _w = jnp.asarray
    def _rec_inputs():
        import jax
        import jax.numpy as jnp
        _gk = jax.random.key(seed)
        x = -0.0003929 + 0.9999 * jax.random.normal(jax.random.fold_in(_gk, 1), (8, 128, 128, 128), jnp.float32)
        return x
    x = _rec_inputs()
    def _L0_conv_setup():
        import jax, jax.numpy as jnp
        import numpy as np
        import math
        B, C, H, W = (8, 128, 128, 128)
        NH = 8
        HD = C // NH
        key = jax.random.key(seed)
        ks = jax.random.split(key, 5)
        s = 0.02
        return {'x': jax.random.normal(ks[0], (B, C, H, W), jnp.float32), 'qkv_w': jax.random.normal(ks[1], (3 * C, C), jnp.float32) * s, 'proj_w': jax.random.normal(ks[2], (C, C), jnp.float32) * s, 'proj_b': jnp.zeros((C,), jnp.float32), 'conv_w': jax.random.normal(ks[3], (C, 1, 3, 3), jnp.float32) * s, 'conv_b': jnp.zeros((C,), jnp.float32), 'ln_g': jnp.ones((C,), jnp.float32), 'ln_b': jnp.zeros((C,), jnp.float32)}
    _L0_conv_all = _L0_conv_setup()
    _L0_conv_in = {k: v for k, v in _L0_conv_all.items() if k in ('qkv_w', 'proj_w', 'proj_b', 'conv_w', 'conv_b', 'ln_g', 'ln_b', )}
    del _L0_conv_all

    def _L1_conv_setup():
        import jax, jax.numpy as jnp
        import numpy as np
        from jax import lax
        DIM = 128
        HEADS = 8
        B, H, W = (8, 128, 128)

        def conv1x1(w, x):
            return jnp.einsum('oc,bchw->bohw', w, x)
        key = jax.random.key(seed)
        ks = jax.random.split(key, 12)
        s = 0.02
        return {'x': jax.random.normal(ks[0], (B, DIM, H, W), dtype=jnp.float32), 'W_qkv': jax.random.normal(ks[1], (3 * DIM, DIM), dtype=jnp.float32) * s, 'W_dw': jax.random.normal(ks[2], (DIM, 1, 3, 3), dtype=jnp.float32) * s, 'W_proj_s': jax.random.normal(ks[3], (DIM, DIM), dtype=jnp.float32) * s, 'scale_s': jnp.ones((HEADS, 1, 1), dtype=jnp.float32), 'W_ff1': jax.random.normal(ks[4], (DIM, DIM), dtype=jnp.float32) * s, 'W_ff2': jax.random.normal(ks[5], (DIM, DIM), dtype=jnp.float32) * s, 'W_proj_f': jax.random.normal(ks[6], (DIM, DIM), dtype=jnp.float32) * s, 'W_gsf': jax.random.normal(ks[7], (DIM, DIM), dtype=jnp.float32) * s, 'b_gsf': jnp.zeros((DIM,), dtype=jnp.float32), 'W_gfs': jax.random.normal(ks[8], (DIM, DIM), dtype=jnp.float32) * s, 'b_gfs': jnp.zeros((DIM,), dtype=jnp.float32)}
    _L1_conv_all = _L1_conv_setup()
    _L1_conv_in = {k: v for k, v in _L1_conv_all.items() if k in ('W_qkv', 'W_dw', 'W_proj_s', 'scale_s', 'W_ff1', 'W_ff2', 'W_proj_f', 'W_gsf', 'b_gsf', 'W_gfs', 'b_gfs', )}
    del _L1_conv_all

    return {
        "x": x,
        "L0_conv_qkv_w": _L0_conv_in["qkv_w"],
        "L0_conv_proj_w": _L0_conv_in["proj_w"],
        "L0_conv_proj_b": _L0_conv_in["proj_b"],
        "L0_conv_conv_w": _L0_conv_in["conv_w"],
        "L0_conv_conv_b": _L0_conv_in["conv_b"],
        "L0_conv_ln_g": _L0_conv_in["ln_g"],
        "L0_conv_ln_b": _L0_conv_in["ln_b"],
        "L1_conv_W_qkv": _L1_conv_in["W_qkv"],
        "L1_conv_W_dw": _L1_conv_in["W_dw"],
        "L1_conv_W_proj_s": _L1_conv_in["W_proj_s"],
        "L1_conv_scale_s": _L1_conv_in["scale_s"],
        "L1_conv_W_ff1": _L1_conv_in["W_ff1"],
        "L1_conv_W_ff2": _L1_conv_in["W_ff2"],
        "L1_conv_W_proj_f": _L1_conv_in["W_proj_f"],
        "L1_conv_W_gsf": _L1_conv_in["W_gsf"],
        "L1_conv_b_gsf": _L1_conv_in["b_gsf"],
        "L1_conv_W_gfs": _L1_conv_in["W_gfs"],
        "L1_conv_b_gfs": _L1_conv_in["b_gfs"],
    }

def reference(x, L0_conv_qkv_w, L0_conv_proj_w, L0_conv_proj_b, L0_conv_conv_w, L0_conv_conv_b, L0_conv_ln_g, L0_conv_ln_b, L1_conv_W_qkv, L1_conv_W_dw, L1_conv_W_proj_s, L1_conv_scale_s, L1_conv_W_ff1, L1_conv_W_ff2, L1_conv_W_proj_f, L1_conv_W_gsf, L1_conv_b_gsf, L1_conv_W_gfs, L1_conv_b_gfs):
    import jax
    import jax.numpy as jnp
    def _L0_conv_ref(x, qkv_w, proj_w, proj_b, conv_w, conv_b, ln_g, ln_b):
        import jax, jax.numpy as jnp
        import numpy as np
        import math
        B, C, H, W = (8, 128, 128, 128)
        NH = 8
        HD = C // NH
        Bx, Cx, Hx, Wx = x.shape
        yc = (jnp.arange(Hx, dtype=jnp.float32) - Hx // 2)[:, None]
        xc = (jnp.arange(Wx, dtype=jnp.float32) - Wx // 2)[None, :]
        rho = jnp.sqrt(xc ** 2 + yc ** 2) / (max(Hx, Wx) / 2)
        theta = (jnp.arctan2(yc + jnp.zeros_like(xc), xc + jnp.zeros_like(yc)) + math.pi) / (2 * math.pi)
        pf = jnp.tile(jnp.stack([rho, theta], axis=0), (Cx // 2, 1, 1))
        e = x + pf[None]
        e = jax.lax.conv_general_dilated(e, conv_w, window_strides=(1, 1), padding='SAME', dimension_numbers=('NCHW', 'OIHW', 'NCHW'), feature_group_count=Cx) + conv_b[None, :, None, None]
        N = Hx * Wx
        xf = e.reshape(Bx, Cx, N).transpose(0, 2, 1)
        mu = xf.mean(-1, keepdims=True)
        var = ((xf - mu) ** 2).mean(-1, keepdims=True)
        xf = (xf - mu) * jax.lax.rsqrt(var + 1e-05) * ln_g + ln_b
        qkv = (xf @ qkv_w.T).reshape(Bx, N, 3, NH, HD).transpose(2, 0, 3, 1, 4)
        q = jax.nn.relu(qkv[0])
        k = jax.nn.relu(qkv[1])
        v = qkv[2]
        k_sum = k.sum(axis=-2, keepdims=True)
        d_inv = 1.0 / jnp.clip((q * k_sum).sum(-1, keepdims=True), 1e-06)
        context = jnp.einsum('bhnd,bhne->bhde', k, v)
        out = jnp.einsum('bhnd,bhde->bhne', q, context) * d_inv
        out = out.transpose(0, 2, 1, 3).reshape(Bx, N, Cx)
        out = out @ proj_w.T + proj_b
        return out.transpose(0, 2, 1).reshape(Bx, Cx, Hx, Wx) + x

    def _L1_conv_ref(x, W_qkv, W_dw, W_proj_s, scale_s, W_ff1, W_ff2, W_proj_f, W_gsf, b_gsf, W_gfs, b_gfs):
        import jax, jax.numpy as jnp
        import numpy as np
        from jax import lax
        DIM = 128
        HEADS = 8
        B, H, W = (8, 128, 128)

        def conv1x1(w, x):
            return jnp.einsum('oc,bchw->bohw', w, x)
        b, c, h, w = x.shape
        head = HEADS
        ch = c // head
        qkv = conv1x1(W_qkv, x)
        q_s, k_s, v_s = jnp.split(qkv, 3, axis=1)
        v_s_conv = lax.conv_general_dilated(v_s, W_dw, window_strides=(1, 1), padding='SAME', feature_group_count=c, dimension_numbers=('NCHW', 'OIHW', 'NCHW'))
        q = q_s.reshape(b, head, ch, h * w)
        k = k_s.reshape(b, head, ch, h * w)
        v = v_s.reshape(b, head, ch, h * w)
        attn = jax.nn.softmax(jnp.einsum('bhcn,bhdn->bhcd', q, k) * scale_s, axis=-1)
        out_s = jnp.einsum('bhcd,bhdn->bhcn', attn, v).reshape(b, c, h, w)
        out_s = conv1x1(W_proj_s, out_s + v_s_conv)
        xf = jnp.fft.rfft2(x, norm='ortho')
        spatial_weights = conv1x1(W_ff2, jax.nn.gelu(conv1x1(W_ff1, x), approximate=False))
        freq_weights = jnp.fft.rfft2(spatial_weights, norm='ortho')
        out_f = jnp.fft.irfft2(xf * freq_weights, s=(h, w), norm='ortho')
        out_f = conv1x1(W_proj_f, out_f)
        gate_f = jax.nn.sigmoid(conv1x1(W_gsf, out_s) + b_gsf[:, None, None])
        gate_s = jax.nn.sigmoid(conv1x1(W_gfs, out_f) + b_gfs[:, None, None])
        return x + out_s * gate_s + out_f * gate_f

    def _gn(v, G=32, eps=1e-5):
        B_, C_, H_, W_ = v.shape
        g = v.reshape(B_, G, C_ // G, H_, W_)
        m = jnp.mean(g, axis=(2, 3, 4), keepdims=True)
        s = jnp.var(g, axis=(2, 3, 4), keepdims=True)
        return ((g - m) / jnp.sqrt(s + eps)).reshape(v.shape)

    def _ln_c(v, eps=1e-6):
        m = jnp.mean(v, axis=1, keepdims=True)
        s = jnp.var(v, axis=1, keepdims=True)
        return (v - m) / jnp.sqrt(s + eps)

    def _ln_t(v, eps=1e-5):
        m = jnp.mean(v, axis=-1, keepdims=True)
        s = jnp.var(v, axis=-1, keepdims=True)
        return (v - m) / jnp.sqrt(s + eps)

    def _to_tokens(v):
        B_, C_, H_, W_ = v.shape
        return v.reshape(B_, C_, H_ * W_).transpose(0, 2, 1)
    def _from_tokens(t, like):
        B_, C_, H_, W_ = like.shape
        return t.transpose(0, 2, 1).reshape(B_, C_, H_, W_)

    x = _L0_conv_ref(x, L0_conv_qkv_w, L0_conv_proj_w, L0_conv_proj_b, L0_conv_conv_w, L0_conv_conv_b, L0_conv_ln_g, L0_conv_ln_b)
    x = _L1_conv_ref(x, L1_conv_W_qkv, L1_conv_W_dw, L1_conv_W_proj_s, L1_conv_scale_s, L1_conv_W_ff1, L1_conv_W_ff2, L1_conv_W_proj_f, L1_conv_W_gsf, L1_conv_b_gsf, L1_conv_W_gfs, L1_conv_b_gfs)
    return x


_drawn_inputs = setup_inputs


def setup_inputs(seed=0):
    import zlib

    import numpy as np

    out = dict(_drawn_inputs(seed))
    spreads = {'L0_conv_proj_b': (0.0, 0.1),
     'L0_conv_conv_b': (0.0, 0.1),
     'L0_conv_ln_g': (1.0, 0.6),
     'L0_conv_ln_b': (0.0, 0.8),
     'L1_conv_scale_s': (1.0, 0.6),
     'L1_conv_b_gsf': (0.0, 0.8),
     'L1_conv_b_gfs': (0.0, 2.0)}
    factors = {'L0_conv_conv_w': 3.945,
     'L1_conv_W_dw': 25.133,
     'L1_conv_W_ff1': 8.0,
     'L1_conv_W_ff2': 7.529,
     'L1_conv_W_proj_f': 6.366,
     'L1_conv_W_gsf': 8.0,
     'L1_conv_W_gfs': 64.0}
    for name, (base, spread) in spreads.items():
        noise = np.random.default_rng([zlib.crc32(name.encode()), seed]).standard_normal(out[name].shape)
        drawn = base * np.exp(spread * noise) if base else spread * noise
        out[name] = jnp.asarray(drawn.astype(out[name].dtype))
    for name, factor in factors.items():
        out[name] = (out[name] * factor).astype(out[name].dtype)
    return out
```

```python
from contextlib import ExitStack

import numpy as np

import concourse.bass as bass
from concourse import mybir

F32 = mybir.dt.float32
ALU = mybir.AluOpType
ACT = mybir.ActivationFunctionType

B, C, H, W = 8, 128, 128, 128
HEADS = 8
HEAD = C // HEADS
PIX = H * W
ROWS = 4
CHUNK = ROWS * W
STEPS = H // ROWS
GROUP = 4
UNROLL = 4
QUADS = STEPS // UNROLL
KW = W // 2 + 1
KI = W // 2 - 1
HALF = H // 2
PAD = W + 2
TAPS = 9
MAPS = 2 * TAPS + 1
CREDIT = 4

LN_EPS = 1e-5
DEN_MIN = 1e-6

SQUARES = ["ident", "center", "head_mask", "head_off", "col_fwd", "row_even", "row_mix", "row_cos", "row_sin", "col_inv"]
WEIGHTS = ["q0", "k0", "v0", "proj0", "q1", "k1", "v1", "proj_s", "ff1", "ff2", "proj_f", "gate_sf", "gate_fs"]
VECTORS = ["proj_b", "conv_b", "ln_g", "ln_b", "b_gsf", "b_gfs"]


def shape_constants():
    f = np.float64
    k = np.arange(128)
    head = k // HEAD
    same = head[:, None] == head[None, :]
    sq = {}
    sq["ident"] = np.eye(C)
    sq["center"] = np.eye(C) - 1.0 / C
    sq["head_mask"] = same
    sq["head_off"] = np.where(same, 0.0, -1e30)
    w, kr, ki = k[:, None].astype(f), np.arange(KW)[None, :], np.arange(1, KI + 1)[None, :]
    sq["col_fwd"] = np.concatenate([np.cos(2 * np.pi * w * kr / W), np.sin(2 * np.pi * w * ki / W)], 1)
    h = np.arange(HALF)[:, None] + 0.5
    cos, sin = np.cos(2 * np.pi * h * k[None, :] / H), np.sin(2 * np.pi * h * k[None, :] / H)
    sq["row_even"] = np.concatenate([cos, -sin], 0)
    sq["row_mix"] = np.concatenate([cos, sin], 0)
    sq["row_cos"] = np.cos(2 * np.pi * k[:, None] * (k[None, :] + 1) / H)
    sq["row_sin"] = np.sin(2 * np.pi * k[:, None] * (k[None, :] + 1) / H)
    scale = 1.0 / np.sqrt(float(PIX)) ** 3
    weight = np.where((kr == 0) | (kr == W // 2), 1.0, 2.0).T * scale
    wc = k[None, :].astype(f)
    sq["col_inv"] = np.concatenate([weight * np.cos(2 * np.pi * kr.T * wc / W),
                                    2 * scale * np.sin(2 * np.pi * ki.T * wc / W)], 0)
    squares = np.stack([sq[n] for n in SQUARES], 1).astype(np.float32)
    parity = np.stack([k % 2 == 0, k % 2 == 1], 1).astype(np.float32)
    head_of = (np.arange(HEADS)[:, None] == head[None, :]).astype(np.float32)
    yc = (np.arange(H, dtype=np.float32) - H // 2)[:, None]
    xc = (np.arange(W, dtype=np.float32) - W // 2)[None, :]
    rho = np.sqrt(xc ** 2 + yc ** 2) / np.float32(max(H, W) / 2)
    theta = (np.arctan2(yc + 0 * xc, xc + 0 * yc) + np.float32(np.pi)) / np.float32(2 * np.pi)
    padded = np.pad(np.stack([rho, theta]), ((0, 0), (1, 1), (1, 1)))
    maps = np.ones((MAPS, H, W), np.float32)
    for t in range(TAPS):
        maps[2 * t:2 * t + 2] = padded[:, t // 3:t // 3 + H, t % 3:t % 3 + W]
    return {"squares": squares, "parity": parity, "head_of": head_of, "head_cols": head_of.T.copy(), "maps": maps.reshape(MAPS, PIX)}


def skewed(eng, stages):
    deepest = max(lag for lag, _ in stages)
    first = -(-deepest // UNROLL)

    def turn(q, w):
        for lag, stage in stages:
            sq, su = q + (w - lag) // UNROLL, (w - lag) % UNROLL
            if isinstance(sq, int) and not 0 <= sq < QUADS:
                continue
            stage(sq, su)

    for q in range(first):
        for w in range(UNROLL):
            turn(q, w)
    with eng.Fori(0, QUADS - first) as p:
        for w in range(UNROLL):
            turn(p + first, w)
    for i in range(deepest):
        turn(QUADS + i // UNROLL, i % UNROLL)


def conv_seq_kernel(nc, x, w, squares_d, parity_d, head_of_d, head_cols_d, maps_d, out):
    ctx = ExitStack()
    with ctx:
        def sb(name, shape, dt=F32):
            return ctx.enter_context(nc.sbuf_tensor(name, shape, dt))

        def sem(name):
            return ctx.enter_context(nc.semaphore(name))

        plane_a = sb("plane_a", [128, H + 2, PAD])
        plane_b = sb("plane_b", [128, H + 2, PAD])
        squares = sb("squares", [128, len(SQUARES), 128])
        weights = sb("weights", [128, len(WEIGHTS), 128])
        ring = sb("ring", [128, 26, 4 * 130])
        v_t = sb("v_t", [128, 2, 4, 129])
        parity = sb("parity", [128, 2])
        head_of = sb("head_of", [HEADS, 128])
        head_cols_t = sb("head_cols", [128, HEADS])
        scale8 = sb("scale8", [HEADS, 1])
        vectors = sb("vectors", [128, len(VECTORS)])
        taps0 = sb("taps0", [128, TAPS])
        taps1 = sb("taps1", [128, TAPS])
        tap_maps_w = sb("tap_maps_w", [128, MAPS])
        tap_maps_t = sb("tap_maps_t", [MAPS, 128])
        eps = sb("eps", [128, 1])
        zeros = sb("zeros", [128, 136])
        ksum = sb("ksum", [128, 1])
        read = sb("read", [128, 136])
        std = sb("std", [128, 2, 4])
        sumsq = sb("sumsq", [128, 2, 4])
        rstd = sb("rstd", [128, 2, 4])
        den = sb("den", [128, 2, 4 * HEADS])
        rden = sb("rden", [128, 2, 4 * HEADS])
        scale_col = sb("scale_col", [128, 1])
        gram = sb("gram", [128, 128])
        gram_k = sb("gram_k", [128, 128])
        scores = sb("scores", [128, 128])
        probs = sb("probs", [128, 128])
        attn = sb("attn", [128, 128])
        peak = sb("peak", [128, 1])
        total = sb("total", [128, 1])
        rtotal = sb("rtotal", [128, 1])
        mix = sb("mix", [128, 128])
        bank = ctx.enter_context(nc.psum_tensor("bank", [128, 8, 512], F32))
        x1_d = nc.dram_tensor("x1_scratch", (STEPS, 128, CHUNK), F32, kind="Internal").ap()
        e0_d = nc.dram_tensor("e0_scratch", (STEPS, 128, CHUNK), F32, kind="Internal").ap()

        head_cols = head_cols_t[:, :]

        def square(name):
            return squares[:, SQUARES.index(name), :]

        def weight(name):
            return weights[:, WEIGHTS.index(name), :]

        def vector(name):
            i = VECTORS.index(name)
            return vectors[:, i:i + 1]

        def flat(slot):
            return ring[:, slot, 0:CHUNK]

        def blocks(slot, width=128):
            return ring[:, slot, 0:4 * width].rearrange("p (b n) -> p b n", n=width)

        def e0(u): return 0 + u % 2
        def part(u): return 2 + u % 2
        def xhat_t(u): return 4 + u % 2
        def xf(u): return 6 + u % 2
        def k_t(u): return 8 + u % 2
        junk = 12

        def q_in(u): return 13 + u % 2
        def out_t(u): return 15 + u % 2
        def out_c(u): return 17 + u % 2
        def x1_out(u): return 19 + u % 2
        def x1_t(u): return 21 + u % 2
        def gelu(u): return 23 + u % 2

        def fold_x(u): return 0 + u % 2
        def fold_s(u): return 2 + u % 2
        def t1x(u): return 4 + u % 2
        def t2x(u): return 6 + u % 2
        def t1s(u): return 8 + u % 2
        def t2s(u): return 10 + u % 2
        def spec_x(u, i): return 12 + i
        def prod(u, i): return 14 + 4 * (u % 2) + i
        def left(u, i): return 22 + 2 * (u % 2) + i

        def x1_in(u): return 0 + u % 4
        def y_in(u): return 4 + u % 2
        def outf_in(u): return 6 + u % 2
        def gate_s(u): return 8 + u % 2
        def conv_v(u): return 10 + u % 2
        def out_s(u): return 12 + u % 2
        def gate_f(u): return 14 + u % 2
        def gated_s(u): return 16 + u % 2
        def base(u): return 18 + u % 2
        def gated_f(u): return 20 + u % 2
        def y_out(u): return 22 + u % 2

        def rows_of(plane, q, u):
            return plane[:, bass.ds(q * (UNROLL * ROWS) + (u * ROWS + 1), ROWS), 1:W + 1]

        def chunk_of(q, u):
            return (q * 2, q + 16, q * 2 + 1, q * -1 + 31)[u]

        def place_of(q, u):
            return (q * 2, q * -1 + 31, q * 2 + 1, q + 16)[u]

        def chunk_rows(plane, n):
            return plane[:, bass.ds(n * ROWS + 1, ROWS), 1:W + 1]

        def in_place(u, k):
            return 3 - k if u % 2 else k

        def tap_rows(plane, q, u, t):
            return plane[:, bass.ds(q * (UNROLL * ROWS) + (u * ROWS + t // 3), ROWS), t % 3:t % 3 + W]

        def image_rows(ap, b, q, u):
            return ap[b].rearrange("c (n m) -> n c m", m=CHUNK)[q * UNROLL + u]

        def four(ap):
            return ap.rearrange("p (r n) -> p r n", r=4)

        loads = sem("loads")
        dve_ready = sem("dve_ready")
        pe_ready = sem("pe_ready")
        act_ready = sem("act_ready")
        stage_sems = {}

        def stage(name):
            stage_sems[name] = sem(name)
            return stage_sems[name]

        e0_made, e0_copied = stage("e0_made"), stage("e0_copied")
        conv0 = stage("conv0")
        centered = stage("centered")
        squared = stage("squared")
        normed_t = stage("normed_t")
        normed = stage("normed")
        scaled = stage("scaled")
        kv_made = stage("kv_made")
        k_done = stage("k_done")
        v_done = stage("v_done")
        q_made = stage("q_made")
        q_done = stage("q_done")
        ctx_added = stage("ctx_added")
        read_made = stage("read_made")
        divided = stage("divided")
        turned = stage("turned")
        out_done = stage("out_done")
        projected = stage("projected")
        x1_done = stage("x1_done")
        x1_turned = stage("x1_turned")
        x1_t_done = stage("x1_t_done")
        gram_added = stage("gram_added")
        ff1_made = stage("ff1_made")
        gelu_done = stage("gelu_done")
        s_made = stage("s_made")
        s_done = stage("s_done")
        folded_x = stage("folded_x")
        folded_s = stage("folded_s")
        cols_made = stage("cols_made")
        split_x = stage("split_x")
        split_s = stage("split_s")
        rows_made = stage("rows_made")
        spec_done = stage("spec_done")
        products = stage("products")
        packed = stage("packed")
        back_made = stage("back_made")
        back_done = stage("back_done")
        v_made = stage("v_made")
        v_saved = stage("v_saved")
        conv1 = stage("conv1")
        outf_turned = stage("outf_turned")
        outf_copied = stage("outf_copied")
        outf_made = stage("outf_made")
        gate_s_done = stage("gate_s_done")
        out_s_made = stage("out_s_made")
        out_s_done = stage("out_s_done")
        gate_f_made = stage("gate_f_made")
        gate_f_done = stage("gate_f_done")
        base_done = stage("base_done")
        gated = stage("gated")
        y_done = stage("y_done")
        dve_chain = sem("dve_chain")
        ln_chain = sem("ln_chain")
        pool_chain = sem("pool_chain")
        small_dve = sem("small_dve")
        small_act = sem("small_act")
        small_pe = sem("small_pe")
        small_chain = sem("small_chain")
        ksum_done = sem("ksum_done")
        edges_clear = sem("edges_clear")
        x_in = [sem(f"x_in{i}") for i in range(2)]
        e0_in = [sem(f"e0_in{i}") for i in range(2)]
        e0_out = [sem(f"e0_out{i}") for i in range(2)]
        q_staged = [sem(f"q_staged{i}") for i in range(2)]
        x1_stored = [sem(f"x1_stored{i}") for i in range(2)]
        x1_t_saved = [sem(f"x1_t_saved{i}") for i in range(2)]
        x1_loaded = [sem(f"x1_loaded{i}") for i in range(4)]
        y_staged = [sem(f"y_staged{i}") for i in range(2)]
        y_stored = [sem(f"y_stored{i}") for i in range(2)]

        def done(eng, s, b, q, u, ago=0):
            eng.wait_ge(s, b * STEPS + q * UNROLL + (u + 1 + CREDIT - ago))

        def all_done(eng, s, b):
            eng.wait_ge(s, b * STEPS + (STEPS + CREDIT))

        def moved(eng, sems, b, q, u, ago=0):
            k = len(sems)
            n = u - ago
            eng.wait_ge(sems[n % k], (b * (STEPS // k) + q * (UNROLL // k) + (n // k + 2)) * 16)

        def all_moved(eng, sems, b):
            whole = (b + 1) * (STEPS // len(sems) * 16) + 16
            if not isinstance(b, int):
                whole = eng.snap(whole)
            for s in sems:
                eng.wait_ge(s, whole)

        def credit(eng, sems, count=CREDIT):
            for s in sems:
                eng.nop(nofuse=True).then_inc(s, count)

        block = ctx.enter_context(nc.Block())
        n_setup = 5 + len(VECTORS) + 3 + len(WEIGHTS)
        nat = plane_b[:, :, :].rearrange("p a b -> p (a b)")[:, 0:13 * 128].rearrange("p (a b) -> p a b", b=128)
        maps = plane_a[0:MAPS, :, :].rearrange("p a b -> p (a b)")

        @block.sync
        def _(sp):
            for sems in (x_in, e0_in, e0_out, q_staged, x1_stored, x1_t_saved, x1_loaded, y_staged, y_stored):
                credit(sp, sems, 16)
            sp.dma_start(squares[:, :, :], squares_d).then_inc(loads, 16)
            sp.dma_start(parity[:, :], parity_d).then_inc(loads, 16)
            sp.dma_start(head_of[:, :], head_of_d).then_inc(loads, 16)
            sp.dma_start(head_cols, head_cols_d).then_inc(loads, 16)
            sp.dma_start(maps[:, 0:PIX], maps_d).then_inc(loads, 16)
            for i, name in enumerate(VECTORS):
                sp.dma_start(vectors[:, i:i + 1], w[name].rearrange("(c o) -> c o", o=1)).then_inc(loads, 16)
            sp.dma_start(scale8[:, :], w["scale_s"].rearrange("h a b -> h (a b)")).then_inc(loads, 16)
            sp.dma_start(taps0[:, :], w["conv_w"].rearrange("c o a b -> c (o a b)")).then_inc(loads, 16)
            sp.dma_start(taps1[:, :], w["W_dw"].rearrange("c o a b -> c (o a b)")).then_inc(loads, 16)
            for i, name in enumerate(WEIGHTS):
                sp.dma_start(nat[:, i, :], w[name]).then_inc(loads, 16)

            def store_e0(q, u):
                done(sp, e0_copied, 0, q, u)
                sp.dma_start(e0_d[q * UNROLL + u], flat(part(u))).then_inc(e0_out[u % 2], 16)

            skewed(sp, [(0, store_e0)])
            all_moved(sp, e0_out, 0)
            sp.wait_ge(dve_ready, 6)

            with sp.Fori(0, B) as b:
                for s in y_staged:
                    sp.wait_ge(s, b * (STEPS // 2 * 16) + 16)

                def load_x(q, u):
                    done(sp, conv0, b, q, u, 3)
                    sp.dma_start(rows_of(plane_b, q, u), four(image_rows(x, b, q, u))).then_inc(x_in[u % 2], 16)

                def load_e0(q, u):
                    done(sp, conv0, b, q, u, 2)
                    sp.dma_start(flat(e0(u)), e0_d[q * UNROLL + u]).then_inc(e0_in[u % 2], 16)

                skewed(sp, [(0, load_x), (1, load_e0)])

                all_done(sp, q_done, b)

                def stage_q(q, u):
                    done(sp, read_made, b, q, u, 2)
                    sp.dma_start(four(flat(q_in(u))), chunk_rows(plane_a, chunk_of(q, u))).then_inc(q_staged[u % 2], 16)

                def store_x1(q, u):
                    done(sp, x1_done, b, q, u)
                    sp.dma_start(x1_d[chunk_of(q, u)], flat(x1_out(u))).then_inc(x1_stored[u % 2], 16)

                def save_x1_t(q, u):
                    done(sp, x1_t_done, b, q, u)
                    sp.dma_start(chunk_rows(plane_b, place_of(q, u)), four(flat(x1_t(u)))).then_inc(x1_t_saved[u % 2], 16)

                skewed(sp, [(0, stage_q), (3, store_x1), (5, save_x1_t)])

                spectra = sp.snap(b * STEPS + (STEPS + CREDIT))
                all_moved(sp, x1_stored, b)
                sp.wait_ge(back_done, spectra)

                def load_x1(q, u):
                    if not (isinstance(q, int) and 4 * q + u < 4):
                        done(sp, base_done, b, q, u, 4)
                    sp.dma_start(flat(x1_in(u)), x1_d[q * UNROLL + u]).then_inc(x1_loaded[u % 4], 16)

                def stage_y(q, u):
                    if not (isinstance(q, int) and 4 * q + u < 2):
                        done(sp, outf_turned, b, q, u, 2)
                    sp.dma_start(four(flat(y_in(u))), rows_of(plane_b, q, u)).then_inc(y_staged[u % 2], 16)

                def store_y(q, u):
                    done(sp, y_done, b, q, u)
                    sp.dma_start(image_rows(out, b, q, u), flat(y_out(u))).then_inc(y_stored[u % 2], 16)

                skewed(sp, [(0, load_x1), (1, stage_y), (5, store_y)])
            all_moved(sp, y_stored, B - 1)

        @block.tensor
        def _(pe):
            mm = nc.tensor.matmul
            credit(pe, [e0_made, centered, normed, kv_made, q_made, ctx_added, read_made, turned, projected,
                        x1_turned, gram_added, ff1_made, s_made, cols_made, rows_made, back_made, v_made,
                        outf_turned, outf_made, out_s_made, gate_f_made])
            pe.wait_ge(loads, 16 * n_setup)
            for i in range(len(WEIGHTS)):
                last = nc.tensor.transpose(bank[:, i // 4, (i % 4) * 128:(i % 4 + 1) * 128], nat[:, i, :], square("ident"))
            last.then_inc(pe_ready, 1)
            pe.wait_ge(dve_ready, 3)
            nc.tensor.transpose(bank[0:MAPS, 4, 0:128], tap_maps_w[:, :], square("ident")).then_inc(pe_ready, 1)
            mm(bank[:, 5, 0:1], head_of[:, :], scale8[:, :], start=True, stop=True).then_inc(pe_ready, 1)
            mm(bank[:, 6, 0:128], nat[:, WEIGHTS.index("proj_f"), :], weight("gate_fs"),
               start=True, stop=True).then_inc(pe_ready, 1)
            pe.wait_ge(dve_ready, 4)

            def make_e0(q, u):
                done(pe, e0_copied, 0, q, u, 2)
                mm(bank[:, u % 2, :], tap_maps_t[:, :], maps[:, bass.ds(q * (UNROLL * CHUNK) + u * CHUNK, CHUNK)],
                   start=True, stop=True).then_inc(e0_made, 1)

            skewed(pe, [(0, make_e0)])
            pe.wait_ge(dve_ready, 6)

            with pe.Fori(0, B) as b:
                def center(q, u):
                    done(pe, conv0, b, q, u)
                    done(pe, normed_t, b, q, u, 2)
                    for k in range(4):
                        last = mm(bank[:, u % 2, k * 128:(k + 1) * 128], flat(part(u))[:, k * 128:(k + 1) * 128],
                                  square("center"), start=True, stop=True)
                    last.then_inc(centered, 1)

                def turn_normed(q, u):
                    done(pe, normed_t, b, q, u)
                    done(pe, scaled, b, q, u, 1)
                    for k in range(4):
                        last = nc.tensor.transpose(bank[:, 2, k * 128:(k + 1) * 128],
                                                   flat(xhat_t(u))[:, k * 128:(k + 1) * 128], square("ident"))
                    last.then_inc(normed, 1)

                def make_kv(q, u):
                    done(pe, scaled, b, q, u)
                    done(pe, k_done, b, q, u, 1)
                    done(pe, v_done, b, q, u, 1)
                    for k in range(4):
                        last = mm(bank[:, 3 + k // 2, (k % 2) * 256:(k % 2 + 1) * 256],
                                  flat(xf(u))[:, k * 128:(k + 1) * 128],
                                  weights[:, 1:3, :].rearrange("p a n -> p (a n)"), start=True, stop=True)
                    last.then_inc(kv_made, 1)

                def make_q(q, u):
                    done(pe, q_done, b, q, u, 1)
                    mm(bank[:, 5, :], weight("q0"), flat(xf(u)), start=True, stop=True).then_inc(q_made, 1)

                def add_context(q, u):
                    done(pe, k_done, b, q, u)
                    done(pe, v_done, b, q, u)
                    for k in range(4):
                        last = mm(bank[:, 6, 0:129], blocks(k_t(u))[:, k, :], v_t[:, u % 2, k, :],
                                  start=False, stop=False)
                    last.then_inc(ctx_added, 1)

                pe.wait_ge(gate_f_done, b * STEPS + CREDIT)
                pe.wait_ge(gated, b * STEPS + CREDIT)
                mm(bank[:, 6, 0:129], zeros[:, 0:128], zeros[:, 0:129], start=True, stop=False)
                skewed(pe, [(0, center), (1, turn_normed), (2, make_kv), (2, make_q), (3, add_context)])
                mm(bank[:, 6, 0:129], zeros[:, 0:128], zeros[:, 0:129], start=False, stop=True).then_inc(small_pe, 1)

                all_done(pe, q_done, b)
                pe.wait_ge(small_dve, b * 8 + 1)

                def read_out(q, u):
                    moved(pe, q_staged, b, q, u)
                    done(pe, divided, b, q, u, 1)
                    for k in range(4):
                        last = mm(bank[:, k // 2, (k % 2) * 256:(k % 2) * 256 + 136],
                                  flat(q_in(u))[:, k * 128:(k + 1) * 128], read[:, :], start=True, stop=True)
                    last.then_inc(read_made, 1)

                def turn_out(q, u):
                    done(pe, divided, b, q, u)
                    done(pe, out_done, b, q, u, 1)
                    for k in range(4):
                        last = nc.tensor.transpose(bank[:, 2, k * 128:(k + 1) * 128],
                                                   flat(out_t(u))[:, k * 128:(k + 1) * 128], square("ident"))
                    last.then_inc(turned, 1)

                def project(q, u):
                    done(pe, out_done, b, q, u)
                    done(pe, x1_done, b, q, u, 1)
                    mm(bank[:, 3, :], weight("proj0"), flat(out_c(u)), start=True, stop=True).then_inc(projected, 1)

                def turn_x1(q, u):
                    done(pe, x1_done, b, q, u)
                    done(pe, x1_t_done, b, q, u, 1)
                    for k in range(4):
                        to = in_place(u, k)
                        last = nc.tensor.transpose(bank[:, 4, to * 128:(to + 1) * 128],
                                                   flat(x1_out(u))[:, k * 128:(k + 1) * 128], square("ident"))
                    last.then_inc(x1_turned, 1)

                def make_ff1(q, u):
                    done(pe, gelu_done, b, q, u, 1)
                    mm(bank[:, 5, :], weight("ff1"), flat(x1_out(u)), start=True, stop=True).then_inc(ff1_made, 1)

                def add_gram(q, u):
                    done(pe, x1_t_done, b, q, u)
                    for k in range(4):
                        y = flat(x1_t(u))[:, k * 128:(k + 1) * 128]
                        last = mm(bank[:, 7, 0:128], y, y, start=False, stop=False)
                    last.then_inc(gram_added, 1)

                def make_s(q, u):
                    done(pe, gelu_done, b, q, u)
                    done(pe, s_done, b, q, u, 1)
                    for k in range(4):
                        to = in_place(u, k)
                        last = mm(bank[:, 6, to * 128:(to + 1) * 128], flat(gelu(u))[:, k * 128:(k + 1) * 128],
                                  weight("ff2"), start=True, stop=True)
                    last.then_inc(s_made, 1)

                mm(bank[:, 7, 0:128], zeros[:, 0:128], zeros[:, 0:128], start=True, stop=False)
                skewed(pe, [(0, read_out), (1, turn_out), (2, project), (3, turn_x1), (3, make_ff1),
                            (4, add_gram), (4, make_s)])
                mm(bank[:, 7, 0:128], zeros[:, 0:128], zeros[:, 0:128], start=False, stop=True).then_inc(small_pe, 1)
                pe.wait_ge(small_dve, b * 8 + 2)
                mm(bank[:, 7, 0:128], gram[:, :], weight("k1"), start=True, stop=True).then_inc(small_pe, 1)
                pe.wait_ge(small_dve, b * 8 + 3)
                mm(bank[:, 7, 0:128], weight("q1"), gram_k[:, :], start=True, stop=True).then_inc(small_pe, 1)
                pe.wait_ge(small_dve, b * 8 + 7)
                mm(bank[:, 7, 0:128], attn[:, :], weight("proj_s"), start=True, stop=True).then_inc(small_pe, 1)

                all_done(pe, s_done, b)

                def columns(q, u):
                    done(pe, folded_x, b, q, u)
                    done(pe, folded_s, b, q, u)
                    done(pe, split_x, b, q, u, 1)
                    done(pe, split_s, b, q, u, 1)
                    for i, slot in enumerate((fold_x(u), fold_s(u))):
                        for k in range(4):
                            last = mm(bank[:, i, k * 128:(k + 1) * 128], flat(slot)[:, k * 128:(k + 1) * 128],
                                      square("col_fwd"), start=True, stop=True)
                    last.then_inc(cols_made, 1)

                def rows(q, u):
                    done(pe, split_x, b, q, u)
                    done(pe, split_s, b, q, u)
                    done(pe, products, b, q, u, 1)
                    for i, (slot, m) in enumerate(((t1x(u), "row_even"), (t2x(u), "row_mix"),
                                                   (t1s(u), "row_even"), (t2s(u), "row_mix"))):
                        last = mm(bank[:, 2 + i, 0:4 * KW], square(m), ring[:, slot, 0:4 * KW], start=True, stop=True)
                    last.then_inc(rows_made, 1)

                def rows_back(q, u):
                    done(pe, packed, b, q, u)
                    done(pe, back_done, b, q, u, 1)
                    for k in range(4):
                        o = bank[:, 6, k * 128:(k + 1) * 128]
                        mm(o, flat(left(u, 0))[:, k * 128:(k + 1) * 128], square("row_cos"), start=True, stop=False)
                        last = mm(o, flat(left(u, 1))[:, k * 128:(k + 1) * 128], square("row_sin"),
                                  start=False, stop=True)
                    last.then_inc(back_made, 1)

                skewed(pe, [(1, rows), (0, columns), (3, rows_back)])

                all_done(pe, back_done, b)
                pe.wait_ge(small_dve, b * 8 + 8)

                def make_v(q, u):
                    moved(pe, x1_loaded, b, q, u)
                    done(pe, v_saved, b, q, u, 1)
                    mm(bank[:, 0, :], weight("v1"), flat(x1_in(u)), start=True, stop=True).then_inc(v_made, 1)

                def columns_back(q, u):
                    moved(pe, y_staged, b, q, u)
                    done(pe, outf_copied, b, q, u, 1)
                    for k in range(4):
                        last = mm(bank[:, 1, k * 128:(k + 1) * 128], flat(y_in(u))[:, k * 128:(k + 1) * 128],
                                  square("col_inv"), start=True, stop=True)
                    last.then_inc(outf_turned, 1)

                def project_f(q, u):
                    done(pe, outf_copied, b, q, u)
                    done(pe, gated, b, q, u, 2)
                    done(pe, gate_s_done, b, q, u, 1)
                    mm(bank[:, 2 + u % 2, :], weight("proj_f"), flat(outf_in(u)), start=True, stop=True)
                    mm(bank[:, 4, :], weight("gate_fs"), flat(outf_in(u)), start=True, stop=True).then_inc(outf_made, 1)

                def project_s(q, u):
                    done(pe, conv1, b, q, u)
                    done(pe, out_s_done, b, q, u, 1)
                    mm(four(bank[:, 5, :]), mix[:, :], rows_of(plane_a, q, u), start=True, stop=False)
                    mm(bank[:, 5, :], weight("proj_s"), flat(conv_v(u)), start=False, stop=True).then_inc(out_s_made, 1)

                def make_gate_f(q, u):
                    done(pe, out_s_done, b, q, u)
                    done(pe, gate_f_done, b, q, u, 1)
                    mm(bank[:, 6, :], weight("gate_sf"), flat(out_s(u)), start=True, stop=True).then_inc(gate_f_made, 1)

                skewed(pe, [(0, make_v), (1, columns_back), (3, make_gate_f), (2, project_f), (2, project_s)])

        @block.scalar
        def _(act):
            op = nc.scalar.activation
            credit(act, [e0_copied, squared, scaled, k_done, v_done, q_done, out_done, x1_t_done, gelu_done, split_x,
                         spec_done, back_done, v_saved, outf_copied, gate_s_done, out_s_done, gate_f_done])

            def copy_e0(q, u):
                done(act, e0_made, 0, q, u)
                moved(act, e0_out, 0, q, u, 2)
                op(flat(part(u)), bank[:, u % 2, :], ACT.Copy).then_inc(e0_copied, 1)

            for q in range(QUADS):
                for u in range(UNROLL):
                    copy_e0(q, u)
            act.wait_ge(dve_ready, 6)

            with act.Fori(0, B) as b:
                def square_up(q, u):
                    done(act, centered, b, q, u)
                    done(act, normed_t, b, q, u, 2)
                    for k in range(4):
                        last = op(ring[:, junk, k * 128:(k + 1) * 128], bank[:, u % 2, k * 128:(k + 1) * 128],
                                  ACT.Square, accum_out=sumsq[:, u % 2, k:k + 1])
                    last.then_inc(ln_chain, 1)
                    act.wait_ge(ln_chain, b * STEPS + q * UNROLL + (u + 1))
                    op(std[:, u % 2, :], sumsq[:, u % 2, :], ACT.Sqrt, bias=eps[:, :], scale=1.0 / C).then_inc(squared, 1)

                def scale_shift(q, u):
                    done(act, normed, b, q, u)
                    done(act, kv_made, b, q, u, 2)
                    done(act, q_made, b, q, u, 2)
                    op(flat(xf(u)), bank[:, 2, :], ACT.Identity, bias=vector("ln_b"), scale=vector("ln_g")).then_inc(scaled, 1)

                def finish_kv(q, u):
                    done(act, kv_made, b, q, u)
                    done(act, ctx_added, b, q, u, 2)
                    kv = bank[:, 3:5, :].rearrange("p a (k n) -> p (a k) n", n=256)
                    op(blocks(k_t(u)), kv[:, :, 0:128], ACT.Relu).then_inc(k_done, 1)
                    op(v_t[:, u % 2, :, 0:128], kv[:, :, 128:256], ACT.Copy).then_inc(v_done, 1)

                def finish_q(q, u):
                    done(act, q_made, b, q, u)
                    op(rows_of(plane_a, q, u), four(bank[:, 5, :]), ACT.Relu).then_inc(q_done, 1)

                skewed(act, [(0, square_up), (1, scale_shift), (2, finish_kv), (2, finish_q)])

                def copy_out(q, u):
                    done(act, turned, b, q, u)
                    done(act, projected, b, q, u, 2)
                    op(flat(out_c(u)), bank[:, 2, :], ACT.Copy).then_inc(out_done, 1)

                def copy_x1_t(q, u):
                    done(act, x1_turned, b, q, u)
                    done(act, gram_added, b, q, u, 2)
                    moved(act, x1_t_saved, b, q, u, 2)
                    op(flat(x1_t(u)), bank[:, 4, :], ACT.Copy).then_inc(x1_t_done, 1)

                def make_gelu(q, u):
                    done(act, ff1_made, b, q, u)
                    done(act, s_made, b, q, u, 2)
                    op(flat(gelu(u)), bank[:, 5, :], ACT.Gelu).then_inc(gelu_done, 1)

                skewed(act, [(1, copy_out), (3, copy_x1_t), (3, make_gelu)])
                act.wait_ge(small_dve, b * 8 + 5)
                op(probs[:, :], scores[:, :], ACT.Exp, bias=peak[:, :], accum_out=total[:, :]).then_inc(small_act, 1)

                act.wait_ge(small_dve, b * 8 + 8)

                def split(q, u):
                    done(act, cols_made, b, q, u)
                    done(act, rows_made, b, q, u, 2)
                    cols = bank[:, 0, :].rearrange("p (k n) -> p k n", n=128)
                    re, im = slice(0, KW), slice(KW, 128)
                    one, two = blocks(t1x(u), KW), blocks(t2x(u), KW)
                    op(one[0:HALF, :, :], cols[0:HALF, :, re], ACT.Copy)
                    op(one[HALF:128, :, 1:KW - 1], cols[HALF:128, :, im], ACT.Copy)
                    op(two[0:HALF, :, 1:KW - 1], cols[0:HALF, :, im], ACT.Copy)
                    op(two[HALF:128, :, :], cols[HALF:128, :, re], ACT.Copy).then_inc(split_x, 1)

                def copy_spec(q, u):
                    done(act, rows_made, b, q, u)
                    done(act, products, b, q, u, 1)
                    op(ring[:, spec_x(u, 0), 0:4 * KW], bank[:, 2, 0:4 * KW], ACT.Copy)
                    op(ring[:, spec_x(u, 1), 0:4 * KW], bank[:, 3, 0:4 * KW], ACT.Copy).then_inc(spec_done, 1)

                def copy_back(q, u):
                    done(act, back_made, b, q, u)
                    group = plane_b[:, 1:H + 1, bass.ds(q * (UNROLL * GROUP) + (u * GROUP + 1), GROUP)]
                    op(group.rearrange("p h c -> p c h"), bank[:, 6, :].rearrange("p (k n) -> p k n", n=128),
                       ACT.Copy).then_inc(back_done, 1)

                skewed(act, [(1, copy_spec), (0, split), (3, copy_back)])

                all_done(act, packed, b)
                act.wait_ge(small_dve, b * 8 + 8)

                def save_v(q, u):
                    done(act, v_made, b, q, u)
                    op(rows_of(plane_a, q, u), four(bank[:, 0, :]), ACT.Copy).then_inc(v_saved, 1)

                def copy_outf(q, u):
                    done(act, outf_turned, b, q, u)
                    done(act, outf_made, b, q, u, 2)
                    op(flat(outf_in(u)), bank[:, 1, :], ACT.Copy).then_inc(outf_copied, 1)

                def finish_gate_s(q, u):
                    done(act, outf_made, b, q, u)
                    done(act, base_done, b, q, u, 2)
                    op(flat(gate_s(u)), bank[:, 4, :], ACT.Sigmoid, bias=vector("b_gfs")).then_inc(gate_s_done, 1)

                def copy_out_s(q, u):
                    done(act, out_s_made, b, q, u)
                    done(act, gate_f_made, b, q, u, 2)
                    done(act, base_done, b, q, u, 2)
                    op(flat(out_s(u)), bank[:, 5, :], ACT.Copy).then_inc(out_s_done, 1)

                def finish_gate_f(q, u):
                    done(act, gate_f_made, b, q, u)
                    done(act, gated, b, q, u, 2)
                    op(flat(gate_f(u)), bank[:, 6, :], ACT.Sigmoid, bias=vector("b_gsf")).then_inc(gate_f_done, 1)

                skewed(act, [(0, save_v), (1, copy_outf), (2, finish_gate_s), (2, copy_out_s), (3, finish_gate_f)])

        def fold(eng, plane, o, q, u):
            c = bass.ds(q * (UNROLL * GROUP) + (u * GROUP + 1), GROUP)
            low = plane[:, 1:HALF + 1, c].rearrange("p h c -> p c h")
            high = plane[:, HALF + 1:H + 1, c].rearrange("p h c -> p c h")
            eng.tensor_tensor(o[:, :, 0:HALF], low, high, ALU.add)
            return eng.tensor_tensor(o[:, :, HALF:128], low, high, ALU.subtract)

        @block.vector
        def _(dve):
            v = nc.vector
            credit(dve, [conv0, normed_t, divided, x1_done, s_done, folded_s, split_s, products, conv1, gated, y_done])
            v.memset(zeros[:, :], 0.0)
            v.memset(eps[:, :], LN_EPS)
            for u in range(2):
                v.memset(v_t[:, u, :, 128:129], 1.0)
            dve.wait_ge(loads, 16 * n_setup)
            for p in range(2):
                v.tensor_scalar(tap_maps_w[:, 0:2 * TAPS].rearrange("p (t e) -> p t e", e=2)[:, :, p], taps0[:, :],
                                parity[:, p:p + 1], None, ALU.mult)
            v.tensor_copy(tap_maps_w[:, 2 * TAPS:MAPS], vector("conv_b")).then_inc(dve_ready, 1)
            dve.wait_ge(pe_ready, 1)
            v.tensor_copy(weights[:, 0:8, :], bank[:, 0:2, :].rearrange("p a (k n) -> p (a k) n", n=128)).then_inc(dve_ready, 1)
            v.tensor_copy(weights[:, 8:13, :], bank[:, 2:4, :].rearrange("p a (k n) -> p (a k) n", n=128)[:, 0:5, :]
                          ).then_inc(dve_ready, 1)
            dve.wait_ge(pe_ready, 4)
            v.tensor_copy(tap_maps_t[:, :], bank[0:MAPS, 4, 0:128]).then_inc(dve_ready, 1)
            v.tensor_copy(scale_col[:, :], bank[:, 5, 0:1])
            v.tensor_copy(weight("gate_fs"), bank[:, 6, 0:128]).then_inc(dve_ready, 1)
            all_done(dve, e0_copied, 0)
            for plane in (plane_a, plane_b):
                v.memset(plane[:, 0, :], 0.0)
                v.memset(plane[:, H + 1, :], 0.0)
                v.memset(plane[:, 1:H + 1, 0:1], 0.0)
                last = v.memset(plane[:, 1:H + 1, W + 1:W + 2], 0.0)
            last.then_inc(dve_ready, 1)

            def conv(plane, taps, slot, seen, finished, start):
                for t in range(TAPS):
                    for half in range(2):
                        r = slice(half * 2, half * 2 + 2)
                        o = four(flat(slot))[:, r, :]
                        src = plane(t)[:, r, :]
                        if t:
                            dve.wait_ge(dve_chain, seen + (2 * (t - 1) + half + 1))
                            ins = v.scalar_tensor_tensor(out=o, in0=src, scalar=taps[:, t:t + 1], in1=o,
                                                         op0=ALU.mult, op1=ALU.add)
                        elif start is not None:
                            ins = v.scalar_tensor_tensor(out=o, in0=src, scalar=taps[:, 0:1], in1=start[:, r, :],
                                                         op0=ALU.mult, op1=ALU.add)
                        else:
                            ins = v.tensor_scalar(o, src, taps[:, 0:1], None, ALU.mult)
                        ins.then_inc(finished if t == TAPS - 1 and half else dve_chain, 1)

            CHAIN = 2 * TAPS - 1

            with dve.Fori(0, B) as b:
                def conv_x(q, u):
                    if isinstance(q, int) and 4 * q + u == 0:
                        moved(dve, x_in, b, q, u)
                    if not (isinstance(q, int) and 4 * q + u == STEPS - 1):
                        moved(dve, x_in, b, q, u, -1)
                    moved(dve, e0_in, b, q, u)
                    done(dve, centered, b, q, u, 2)
                    seen = b * (2 * STEPS * CHAIN) + q * (UNROLL * CHAIN) + u * CHAIN
                    conv(lambda t: tap_rows(plane_b, q, u, t), taps0, part(u), seen, conv0, four(flat(e0(u))))

                def normalize(q, u):
                    done(dve, squared, b, q, u)
                    v.reciprocal(rstd[:, u % 2, :], std[:, u % 2, :]).then_inc(small_chain, 1)
                    dve.wait_ge(small_chain, b * (3 * STEPS) + q * UNROLL + (u + 1))
                    done(dve, normed, b, q, u, 2)
                    v.tensor_tensor(blocks(xhat_t(u)), bank[:, u % 2, :].rearrange("p (k n) -> p k n", n=128),
                                    rstd[:, u % 2, :].unsqueeze(2).broadcast_to([128, 4, 128]), ALU.mult).then_inc(normed_t, 1)

                skewed(dve, [(1, conv_x), (2, normalize)])
                dve.wait_ge(small_pe, b * 5 + 1)
                v.tensor_tensor(read[:, 0:128], bank[:, 6, 0:128], square("head_mask"), ALU.mult)
                v.tensor_copy(ksum[:, :], bank[:, 6, 128:129]).then_inc(ksum_done, 1)
                dve.wait_ge(ksum_done, b + 1)
                v.tensor_scalar(read[:, 128:136], head_cols, ksum[:, :], None, ALU.mult).then_inc(small_dve, 1)

                def divide(q, u):
                    done(dve, read_made, b, q, u)
                    n = bank[:, 0:2, :].rearrange("p a (k n) -> p (a k) n", n=256)
                    d = den[:, u % 2, :].rearrange("p (k h) -> p k h", h=HEADS)
                    v.tensor_scalar(d, n[:, :, 128:136], DEN_MIN, None, ALU.max).then_inc(small_chain, 1)
                    dve.wait_ge(small_chain, b * (3 * STEPS) + q * (2 * UNROLL) + (STEPS + 2 * u + 1))
                    v.reciprocal(rden[:, u % 2, :], den[:, u % 2, :]).then_inc(small_chain, 1)
                    dve.wait_ge(small_chain, b * (3 * STEPS) + q * (2 * UNROLL) + (STEPS + 2 * u + 2))
                    done(dve, turned, b, q, u, 2)
                    r = rden[:, u % 2, :].rearrange("p (k h) -> p k h", h=HEADS)
                    v.tensor_tensor(blocks(out_t(u)).rearrange("p k (h d) -> p k h d", d=HEAD),
                                    n[:, :, 0:128].rearrange("p k (h d) -> p k h d", d=HEAD),
                                    r.unsqueeze(3).broadcast_to([128, 4, HEADS, HEAD]), ALU.mult).then_inc(divided, 1)

                def add_x(q, u):
                    done(dve, projected, b, q, u)
                    done(dve, ff1_made, b, q, u, 2)
                    done(dve, x1_turned, b, q, u, 2)
                    moved(dve, x1_stored, b, q, u, 2)
                    v.scalar_tensor_tensor(out=four(flat(x1_out(u))), in0=four(bank[:, 3, :]), scalar=vector("proj_b"),
                                           in1=chunk_rows(plane_b, chunk_of(q, u)), op0=ALU.add, op1=ALU.add).then_inc(x1_done, 1)

                def save_s(q, u):
                    done(dve, s_made, b, q, u)
                    if u == 1:
                        moved(dve, q_staged, b, q, u, -2)
                    v.tensor_copy(chunk_rows(plane_a, place_of(q, u)), four(bank[:, 6, :])).then_inc(s_done, 1)

                skewed(dve, [(0, divide), (2, add_x), (4, save_s)])
                dve.wait_ge(small_pe, b * 5 + 2)
                v.tensor_copy(gram[:, :], bank[:, 7, 0:128]).then_inc(small_dve, 1)
                dve.wait_ge(small_pe, b * 5 + 3)
                v.tensor_copy(gram_k[:, :], bank[:, 7, 0:128]).then_inc(small_dve, 1)
                dve.wait_ge(small_pe, b * 5 + 4)
                v.scalar_tensor_tensor(out=scores[:, :], in0=bank[:, 7, 0:128], scalar=scale_col[:, :],
                                       in1=square("head_off"), op0=ALU.mult, op1=ALU.add).then_inc(small_dve, 1)
                dve.wait_ge(small_dve, b * 8 + 4)
                v.tensor_reduce(peak[:, :], scores[:, :], mybir.AxisListType.X, ALU.max, negate=True).then_inc(small_dve, 1)
                dve.wait_ge(small_act, b + 1)
                v.reciprocal(rtotal[:, :], total[:, :]).then_inc(small_dve, 1)
                dve.wait_ge(small_dve, b * 8 + 6)
                v.tensor_scalar(attn[:, :], probs[:, :], rtotal[:, :], None, ALU.mult).then_inc(small_dve, 1)
                dve.wait_ge(small_pe, b * 5 + 5)
                v.tensor_copy(mix[:, :], bank[:, 7, 0:128]).then_inc(small_dve, 1)

                all_done(dve, s_done, b)
                all_done(dve, gram_added, b)
                all_done(dve, s_made, b)
                all_moved(dve, x1_t_saved, b)
                all_moved(dve, x1_stored, b)

                def clear_edges():
                    for u in range(2):
                        for one, two in ((t1x(u), t2x(u)), (t1s(u), t2s(u))):
                            v.memset(blocks(one, KW)[HALF:128, :, 0:KW:KW - 1], 0.0)
                            last = v.memset(blocks(two, KW)[0:HALF, :, 0:KW:KW - 1], 0.0)
                    last.then_inc(edges_clear, 1)

                clear_edges()

                def fold_up_s(q, u):
                    done(dve, cols_made, b, q, u, 2)
                    fold(v, plane_a, blocks(fold_s(u)), q, u).then_inc(folded_s, 1)

                def split_up_s(q, u):
                    done(dve, cols_made, b, q, u)
                    done(dve, rows_made, b, q, u, 2)
                    cols = bank[:, 1, :].rearrange("p (k n) -> p k n", n=128)
                    re, im = slice(0, KW), slice(KW, 128)
                    one, two = blocks(t1s(u), KW), blocks(t2s(u), KW)
                    v.tensor_copy(one[0:HALF, :, :], cols[0:HALF, :, re])
                    v.tensor_copy(one[HALF:128, :, 1:KW - 1], cols[HALF:128, :, im])
                    v.tensor_copy(two[0:HALF, :, 1:KW - 1], cols[0:HALF, :, im])
                    v.tensor_copy(two[HALF:128, :, :], cols[HALF:128, :, re]).then_inc(split_s, 1)

                def multiply(q, u):
                    done(dve, spec_done, b, q, u)
                    done(dve, packed, b, q, u, 2)
                    for i, (xs, ss) in enumerate(((0, 4), (1, 5), (0, 5), (1, 4))):
                        last = v.tensor_tensor(ring[:, prod(u, i), 0:4 * KW], ring[:, spec_x(u, xs), 0:4 * KW],
                                               bank[:, ss, 0:4 * KW], ALU.mult)
                    last.then_inc(products, 1)

                skewed(dve, [(0, fold_up_s), (2, multiply), (1, split_up_s)])

                all_done(dve, packed, b)
                all_done(dve, back_made, b)

                def conv_of_v(q, u):
                    if isinstance(q, int) and 4 * q + u == STEPS - 1:
                        done(dve, v_saved, b, q, u)
                    else:
                        done(dve, v_saved, b, q, u, -1)
                    done(dve, out_s_made, b, q, u, 2)
                    seen = b * (2 * STEPS * CHAIN) + q * (UNROLL * CHAIN) + (u * CHAIN + STEPS * CHAIN)
                    conv(lambda t: tap_rows(plane_a, q, u, t), taps1, conv_v(u), seen, conv1, None)

                def gate_out_f(q, u):
                    done(dve, gate_f_done, b, q, u)
                    done(dve, y_done, b, q, u, 2)
                    v.tensor_tensor(flat(gated_f(u)), bank[:, 2 + u % 2, :], flat(gate_f(u)), ALU.mult).then_inc(gated, 1)

                def finish(q, u):
                    done(dve, gated, b, q, u)
                    done(dve, base_done, b, q, u)
                    moved(dve, y_stored, b, q, u, 2)
                    v.tensor_tensor(flat(y_out(u)), flat(gated_f(u)), flat(base(u)), ALU.add).then_inc(y_done, 1)

                skewed(dve, [(1, conv_of_v), (3, gate_out_f), (4, finish)])

        @block.gpsimd
        def _(pool):
            g = nc.gpsimd
            credit(pool, [folded_x, packed, base_done])
            with pool.Fori(0, B) as b:
                pool.wait_ge(edges_clear, b + 1)

                def fold_up_x(q, u):
                    done(pool, cols_made, b, q, u, 2)
                    fold(g, plane_b, blocks(fold_x(u)), q, u).then_inc(folded_x, 1)

                def pack(q, u):
                    done(pool, products, b, q, u)
                    done(pool, back_made, b, q, u, 2)
                    rr, ii, ri, ir = (blocks(prod(u, i), KW) for i in range(4))
                    one, two = blocks(left(u, 0)), blocks(left(u, 1))
                    mid = slice(1, KW - 1)
                    g.tensor_tensor(one[:, :, 0:KW], rr, ii, ALU.subtract)
                    g.tensor_tensor(one[:, :, KW:128], ri[:, :, mid], ir[:, :, mid], ALU.add)
                    g.tensor_tensor(two[:, :, 0:KW], ri, ir, ALU.add)
                    g.tensor_tensor(two[:, :, KW:128], ii[:, :, mid], rr[:, :, mid], ALU.subtract).then_inc(packed, 1)

                skewed(pool, [(0, fold_up_x), (2, pack)])

                all_done(pool, back_made, b)

                def gate_out_s(q, u):
                    done(pool, gate_s_done, b, q, u)
                    done(pool, out_s_done, b, q, u)
                    done(pool, y_done, b, q, u, 2)
                    g.tensor_tensor(flat(gated_s(u)), flat(out_s(u)), flat(gate_s(u)), ALU.mult).then_inc(pool_chain, 1)
                    pool.wait_ge(pool_chain, b * STEPS + q * UNROLL + (u + 1))
                    moved(pool, x1_loaded, b, q, u)
                    g.tensor_tensor(flat(base(u)), flat(gated_s(u)), flat(x1_in(u)), ALU.add).then_inc(base_done, 1)

                skewed(pool, [(1, gate_out_s)])


_ARGS = {
    "proj_b": "L0_conv_proj_b", "conv_b": "L0_conv_conv_b", "ln_g": "L0_conv_ln_g", "ln_b": "L0_conv_ln_b",
    "b_gsf": "L1_conv_b_gsf", "b_gfs": "L1_conv_b_gfs", "scale_s": "L1_conv_scale_s",
    "conv_w": "L0_conv_conv_w", "W_dw": "L1_conv_W_dw", "proj0": "L0_conv_proj_w", "proj_s": "L1_conv_W_proj_s",
    "ff1": "L1_conv_W_ff1", "ff2": "L1_conv_W_ff2", "proj_f": "L1_conv_W_proj_f", "gate_sf": "L1_conv_W_gsf",
    "gate_fs": "L1_conv_W_gfs",
}


def kernel(**inputs):
    import concourse.bacc as bacc
    from concourse.bass_utils import run_bass_kernel_spmd

    nc = bacc.Bacc("TRN2", target_bir_lowering=False, num_devices=1)
    arrays = {name: np.ascontiguousarray(a) for name, a in inputs.items()}
    arrays["x"] = arrays["x"].reshape(-1, C, PIX)
    arrays.update(shape_constants())
    aps = {name: nc.dram_tensor("in_" + name, a.shape, F32, kind="ExternalInput").ap() for name, a in arrays.items()}
    out = nc.dram_tensor("out", (B, C, PIX), F32, kind="ExternalOutput").ap()
    w = {short: aps[name] for short, name in _ARGS.items()}
    for i, part in enumerate("qkv"):
        w[f"{part}0"] = aps["L0_conv_qkv_w"][i * C:(i + 1) * C, :]
        w[f"{part}1"] = aps["L1_conv_W_qkv"][i * C:(i + 1) * C, :]
    conv_seq_kernel(nc, aps["x"], w, aps["squares"], aps["parity"], aps["head_of"], aps["head_cols"], aps["maps"], out)
    result = run_bass_kernel_spmd(nc, [{"in_" + name: a for name, a in arrays.items()}], core_ids=[0])
    return result.results[0]["out"].reshape(B, C, H, W)
```

```python
from contextlib import ExitStack

import numpy as np

import concourse.bass as bass
from concourse import mybir

F32 = mybir.dt.float32
ALU = mybir.AluOpType
ACT = mybir.ActivationFunctionType

B, C, H, W = 8, 128, 128, 128
HEADS = 8
HEAD = C // HEADS
PIX = H * W
ROWS = 4
CHUNK = ROWS * W
STEPS = H // ROWS
GROUP = 4
UNROLL = 4
QUADS = STEPS // UNROLL
PAIRS = STEPS // 2
KW = W // 2 + 1
KI = W // 2 - 1
HALF = H // 2
PAD = W + 2
TAPS = 9
FIRST_TAPS = 4
DVE_TAPS = 7
MAPS = 2 * TAPS + 1
CREDIT = 4

LN_EPS = 1e-5
DEN_MIN = 1e-6

SQUARES = ["ident", "center", "head_mask", "head_off", "col_fwd", "row_even", "row_mix", "row_cos", "row_sin", "col_inv"]
WEIGHTS = ["q0", "k0", "v0", "proj0", "q1", "k1", "v1", "proj_s", "ff1", "ff2", "proj_f", "gate_sf", "gate_fs"]
VECTORS = ["proj_b", "conv_b", "ln_g", "ln_b", "b_gsf", "b_gfs"]


def shape_constants():
    f = np.float64
    k = np.arange(128)
    head = k // HEAD
    same = head[:, None] == head[None, :]
    sq = {}
    sq["ident"] = np.eye(C)
    sq["center"] = np.eye(C) - 1.0 / C
    sq["head_mask"] = same
    sq["head_off"] = np.where(same, 0.0, -1e30)
    w, kr, ki = k[:, None].astype(f), np.arange(KW)[None, :], np.arange(1, KI + 1)[None, :]
    sq["col_fwd"] = np.concatenate([np.cos(2 * np.pi * w * kr / W), np.sin(2 * np.pi * w * ki / W)], 1)
    h = np.arange(HALF)[:, None] + 0.5
    cos, sin = np.cos(2 * np.pi * h * k[None, :] / H), np.sin(2 * np.pi * h * k[None, :] / H)
    sq["row_even"] = np.concatenate([cos, -sin], 0)
    sq["row_mix"] = np.concatenate([cos, sin], 0)
    sq["row_cos"] = np.cos(2 * np.pi * k[:, None] * (k[None, :] + 1) / H)
    sq["row_sin"] = np.sin(2 * np.pi * k[:, None] * (k[None, :] + 1) / H)
    scale = 1.0 / np.sqrt(float(PIX)) ** 3
    weight = np.where((kr == 0) | (kr == W // 2), 1.0, 2.0).T * scale
    wc = k[None, :].astype(f)
    sq["col_inv"] = np.concatenate([weight * np.cos(2 * np.pi * kr.T * wc / W),
                                    2 * scale * np.sin(2 * np.pi * ki.T * wc / W)], 0)
    squares = np.stack([sq[n] for n in SQUARES], 1).astype(np.float32)
    parity = np.stack([k % 2 == 0, k % 2 == 1], 1).astype(np.float32)
    head_of = (np.arange(HEADS)[:, None] == head[None, :]).astype(np.float32)
    yc = (np.arange(H, dtype=np.float32) - H // 2)[:, None]
    xc = (np.arange(W, dtype=np.float32) - W // 2)[None, :]
    rho = np.sqrt(xc ** 2 + yc ** 2) / np.float32(max(H, W) / 2)
    theta = (np.arctan2(yc + 0 * xc, xc + 0 * yc) + np.float32(np.pi)) / np.float32(2 * np.pi)
    padded = np.pad(np.stack([rho, theta]), ((0, 0), (1, 1), (1, 1)))
    maps = np.ones((MAPS, H, W), np.float32)
    for t in range(TAPS):
        maps[2 * t:2 * t + 2] = padded[:, t // 3:t // 3 + H, t % 3:t % 3 + W]
    return {"squares": squares, "parity": parity, "head_of": head_of, "head_cols": head_of.T.copy(), "maps": maps.reshape(MAPS, PIX)}


def skewed(eng, stages):
    deepest = max(lag for lag, _ in stages)
    first = -(-deepest // UNROLL)

    def turn(q, w):
        for lag, stage in stages:
            sq, su = q + (w - lag) // UNROLL, (w - lag) % UNROLL
            if isinstance(sq, int) and not 0 <= sq < QUADS:
                continue
            stage(sq, su)

    for q in range(first):
        for w in range(UNROLL):
            turn(q, w)
    with eng.Fori(0, QUADS - first) as p:
        for w in range(UNROLL):
            turn(p + first, w)
    for i in range(deepest):
        turn(QUADS + i // UNROLL, i % UNROLL)


def conv_seq_kernel(nc, x, w, squares_d, parity_d, head_of_d, head_cols_d, maps_d, out):
    ctx = ExitStack()
    with ctx:
        def sb(name, shape, dt=F32):
            return ctx.enter_context(nc.sbuf_tensor(name, shape, dt))

        def sem(name):
            return ctx.enter_context(nc.semaphore(name))

        plane_a = sb("plane_a", [128, H + 2, PAD])
        plane_b = sb("plane_b", [128, H + 2, PAD])
        squares = sb("squares", [128, len(SQUARES), 128])
        weights = sb("weights", [128, len(WEIGHTS), 128])
        ring = sb("ring", [128, 32, CHUNK])
        v_t = sb("v_t", [128, 2, 4, 129])
        parity = sb("parity", [128, 2])
        head_of = sb("head_of", [HEADS, 128])
        head_cols_t = sb("head_cols", [128, HEADS])
        scale8 = sb("scale8", [HEADS, 1])
        vectors = sb("vectors", [128, len(VECTORS)])
        taps0 = sb("taps0", [128, TAPS])
        taps1 = sb("taps1", [128, TAPS])
        tap_maps_w = sb("tap_maps_w", [128, MAPS])
        tap_maps_t = sb("tap_maps_t", [MAPS, 128])
        eps = sb("eps", [128, 1])
        zeros = sb("zeros", [128, 136])
        ksum = sb("ksum", [128, 1])
        read = sb("read", [128, 136])
        std = sb("std", [128, 2, 4])
        sumsq = sb("sumsq", [128, 2, 4])
        rstd = sb("rstd", [128, 2, 4])
        den = sb("den", [128, 2, 4 * HEADS])
        rden = sb("rden", [128, 2, 4 * HEADS])
        scale_col = sb("scale_col", [128, 1])
        gram = sb("gram", [128, 128])
        gram_k = sb("gram_k", [128, 128])
        scores = sb("scores", [128, 128])
        probs = sb("probs", [128, 128])
        attn = sb("attn", [128, 128])
        peak = sb("peak", [128, 1])
        total = sb("total", [128, 1])
        rtotal = sb("rtotal", [128, 1])
        mix = sb("mix", [128, 128])
        bank = ctx.enter_context(nc.psum_tensor("bank", [128, 8, 512], F32))
        e0_d = nc.dram_tensor("e0_scratch", (128, PIX), F32, kind="Internal").ap()
        x1_d = nc.dram_tensor("x1_scratch", (STEPS, 128, CHUNK), F32, kind="Internal").ap()

        head_cols = head_cols_t[:, :]

        def square(name):
            return squares[:, SQUARES.index(name), :]

        def weight(name):
            return weights[:, WEIGHTS.index(name), :]

        def vector(name):
            i = VECTORS.index(name)
            return vectors[:, i:i + 1]

        def flat(slot):
            return ring[:, slot, 0:CHUNK]

        def blocks(slot, width=128):
            return ring[:, slot, 0:4 * width].rearrange("p (b n) -> p b n", n=width)

        def e0(u): return 0 + u % 4
        junk = 4
        def part(u): return 8 + u % 4
        def xhat_t(u): return 12 + u % 2
        def seeds(u): return 14 + u % 4
        def xf(u): return 18 + u % 2
        def k_t(u): return 20 + u % 2
        def tap_a(u): return 26 + u % 4
        def tap_b(u): return (30, 31, 6, 7)[u % 4]

        def x1_out(u): return 20 + u % 2
        def q_in(u): return 22 + u % 2
        def out_t(u): return 24 + u % 2
        def x1_t(u): return 26 + u % 2
        def out_c(u): return 28 + u % 2
        def gelu(u): return 30 + u % 2

        def fold_x(u): return 0 + u % 2
        def fold_s(u): return 2 + u % 2
        def t1x(u): return 4 + u % 2
        def t2x(u): return 6 + u % 2
        def t1s(u): return 8 + u % 2
        def t2s(u): return 10 + u % 2
        def spec_x(i): return 12 + i
        def prod(u, i): return 14 + 4 * (u % 2) + i
        def left(u, i): return 22 + 2 * (u % 2) + i

        def x1_in(u): return 0 + u % 4
        def x1_again(u): return 4 + u % 2
        def y_in(u): return 6 + u % 2
        def outf_in(u): return 8 + u % 2
        def conv_v(u): return 10 + u % 4
        def gate_s(u): return 14 + u % 2
        def out_s(u): return 16 + u % 2
        def gate_f(u): return 18 + u % 2
        def base(u): return 20 + u % 2
        def y_out(u): return 22 + u % 4
        def seed_v(u): return 26 + u % 4
        def tap_v(u): return 30 + u % 2

        def rows_of(plane, q, u):
            return plane[:, bass.ds(q * (UNROLL * ROWS) + (u * ROWS + 1), ROWS), 1:W + 1]

        def chunk_of(q, u):
            return (q * 2, q + 16, q * 2 + 1, q * -1 + 31)[u]

        def place_of(q, u):
            return (q * 2, q * -1 + 31, q * 2 + 1, q + 16)[u]

        def chunk_rows(plane, n):
            return plane[:, bass.ds(n * ROWS + 1, ROWS), 1:W + 1]

        def in_place(u, k):
            return 3 - k if u % 2 else k

        def tap_rows(plane, q, u, t):
            return plane[:, bass.ds(q * (UNROLL * ROWS) + (u * ROWS + t // 3), ROWS), t % 3:t % 3 + W]

        def load_piece(sp, b, q, u):
            piece = 4 * q + u if isinstance(q, int) else None
            above, below = int(piece != 0), int(piece != STEPS - 2)
            start, n = q * (UNROLL * ROWS) + (u * ROWS + above), 2 * ROWS - above + below
            sp.dma_start(plane_b[:, bass.ds(start + 1, n), 1:W + 1],
                         x[b].rearrange("c (h w) -> c h w", w=W)[:, bass.ds(start, n), :]).then_inc(x_in[u // 2], 16)

        def pair_of(ap, q, u):
            return ap.rearrange("c (n m) -> n c m", m=2 * CHUNK)[q * (UNROLL // 2) + u // 2]

        def image_rows(ap, b, q, u):
            return ap[b].rearrange("c (n m) -> n c m", m=CHUNK)[q * UNROLL + u]

        def four(ap):
            return ap.rearrange("p (r n) -> p r n", r=4)

        loads = sem("loads")
        dve_ready = sem("dve_ready")
        pe_ready = sem("pe_ready")
        act_ready = sem("act_ready")
        stage_sems = {}

        def stage(name):
            stage_sems[name] = sem(name)
            return stage_sems[name]

        e0_made, e0_copied = stage("e0_made"), stage("e0_copied")
        last_taps = stage("last_taps")
        seeded = stage("seeded")
        conv0 = stage("conv0")
        centered = stage("centered")
        squared = stage("squared")
        normed_t = stage("normed_t")
        normed = stage("normed")
        scaled = stage("scaled")
        kv_made = stage("kv_made")
        k_done = stage("k_done")
        v_done = stage("v_done")
        q_made = stage("q_made")
        q_done = stage("q_done")
        ctx_added = stage("ctx_added")
        read_made = stage("read_made")
        divided = stage("divided")
        turned = stage("turned")
        out_done = stage("out_done")
        projected = stage("projected")
        x1_done = stage("x1_done")
        x1_turned = stage("x1_turned")
        x1_t_done = stage("x1_t_done")
        gram_added = stage("gram_added")
        ff1_made = stage("ff1_made")
        gelu_done = stage("gelu_done")
        s_made = stage("s_made")
        s_done = stage("s_done")
        folded_x = stage("folded_x")
        folded_s = stage("folded_s")
        cols_made = stage("cols_made")
        split_x = stage("split_x")
        split_s = stage("split_s")
        rows_made = stage("rows_made")
        spec_done = stage("spec_done")
        products = stage("products")
        packed = stage("packed")
        back_made = stage("back_made")
        back_done = stage("back_done")
        v_made = stage("v_made")
        v_saved = stage("v_saved")
        last_taps_v = stage("last_taps_v")
        seeded_v = stage("seeded_v")
        conv1 = stage("conv1")
        outf_turned = stage("outf_turned")
        outf_copied = stage("outf_copied")
        outf_made = stage("outf_made")
        gate_s_done = stage("gate_s_done")
        out_s_made = stage("out_s_made")
        out_s_done = stage("out_s_done")
        gate_f_made = stage("gate_f_made")
        gate_f_done = stage("gate_f_done")
        base_done = stage("base_done")
        gated = stage("gated")
        y_done = stage("y_done")
        dve_chain = sem("dve_chain")
        ln_chain = sem("ln_chain")
        pool_chain = sem("pool_chain")
        seed_chain = sem("seed_chain")
        small_dve = sem("small_dve")
        small_act = sem("small_act")
        small_pe = sem("small_pe")
        small_chain = sem("small_chain")
        ksum_done = sem("ksum_done")
        edges_clear = sem("edges_clear")
        x_in = [sem(f"x_in{i}") for i in range(2)]
        e0_in = [sem(f"e0_in{i}") for i in range(2)]
        e0_out = [sem(f"e0_out{i}") for i in range(2)]
        q_staged = [sem(f"q_staged{i}") for i in range(2)]
        x1_stored = [sem(f"x1_stored{i}") for i in range(2)]
        x1_t_saved = [sem(f"x1_t_saved{i}") for i in range(2)]
        x1_loaded = [sem(f"x1_loaded{i}") for i in range(4)]
        x1_reloaded = [sem(f"x1_reloaded{i}") for i in range(2)]
        y_staged = [sem(f"y_staged{i}") for i in range(2)]
        y_stored = [sem(f"y_stored{i}") for i in range(4)]

        def done(eng, s, b, q, u, ago=0):
            eng.wait_ge(s, b * STEPS + q * UNROLL + (u + 1 + CREDIT - ago))

        def pair_done(eng, s, b, q, u, ago=0):
            eng.wait_ge(s, b * PAIRS + q * (UNROLL // 2) + (u // 2 + 1 + CREDIT - ago))

        def pair_moved(eng, sems, b, q, u, ago=0):
            n = u // 2 - ago
            eng.wait_ge(sems[n % 2], (b * (PAIRS // 2) + q + (n // 2 + 2)) * 16)

        def all_done(eng, s, b):
            eng.wait_ge(s, b * STEPS + (STEPS + CREDIT))

        def moved(eng, sems, b, q, u, ago=0):
            k = len(sems)
            n = u - ago
            eng.wait_ge(sems[n % k], (b * (STEPS // k) + q * (UNROLL // k) + (n // k + 2)) * 16)

        def all_moved(eng, sems, b):
            whole = (b + 1) * (STEPS // len(sems) * 16) + 16
            if not isinstance(b, int):
                whole = eng.snap(whole)
            for s in sems:
                eng.wait_ge(s, whole)

        def credit(eng, sems, count=CREDIT):
            for s in sems:
                eng.nop(nofuse=True).then_inc(s, count)

        block = ctx.enter_context(nc.Block())
        n_setup = 5 + len(VECTORS) + 3 + len(WEIGHTS)
        nat = plane_b[:, :, :].rearrange("p a b -> p (a b)")[:, 0:13 * 128].rearrange("p (a b) -> p a b", b=128)
        maps = plane_a[0:MAPS, :, :].rearrange("p a b -> p (a b)")

        @block.sync
        def _(sp):
            for sems in (x_in, e0_in, e0_out, q_staged, x1_stored, x1_t_saved, x1_loaded, x1_reloaded, y_staged, y_stored):
                credit(sp, sems, 16)
            sp.dma_start(squares[:, :, :], squares_d).then_inc(loads, 16)
            sp.dma_start(parity[:, :], parity_d).then_inc(loads, 16)
            sp.dma_start(head_of[:, :], head_of_d).then_inc(loads, 16)
            sp.dma_start(head_cols, head_cols_d).then_inc(loads, 16)
            sp.dma_start(maps[:, 0:PIX], maps_d).then_inc(loads, 16)
            for i, name in enumerate(VECTORS):
                sp.dma_start(vectors[:, i:i + 1], w[name].rearrange("(c o) -> c o", o=1)).then_inc(loads, 16)
            sp.dma_start(scale8[:, :], w["scale_s"].rearrange("h a b -> h (a b)")).then_inc(loads, 16)
            sp.dma_start(taps0[:, :], w["conv_w"].rearrange("c o a b -> c (o a b)")).then_inc(loads, 16)
            sp.dma_start(taps1[:, :], w["W_dw"].rearrange("c o a b -> c (o a b)")).then_inc(loads, 16)
            for i, name in enumerate(WEIGHTS):
                sp.dma_start(nat[:, i, :], w[name]).then_inc(loads, 16)

            def store_e0(q, u):
                done(sp, e0_copied, 0, q, u)
                sp.dma_start(e0_d.rearrange("c (n m) -> n c m", m=CHUNK)[q * UNROLL + u], flat(part(u))).then_inc(e0_out[u % 2], 16)

            skewed(sp, [(0, store_e0)])
            all_moved(sp, e0_out, 0)
            sp.wait_ge(dve_ready, 6)

            def load_first(b):
                for u in (0, 2):
                    load_piece(sp, b, 0, u)
                    sp.dma_start(ring[:, e0(u):e0(u) + 2, 0:CHUNK], pair_of(e0_d, 0, u).rearrange(
                        "c (a n) -> c a n", a=2)).then_inc(e0_in[u // 2], 16)

            load_first(0)

            with sp.Fori(0, B) as b:
                def load_x(q, u):
                    if u % 2 == 0 and not (isinstance(q, int) and q == 0):
                        done(sp, last_taps, b, q, u, 4)
                        load_piece(sp, b, q, u)

                def load_e0(q, u):
                    if u % 2 == 0 and not (isinstance(q, int) and q == 0):
                        done(sp, seeded, b, q, u, 3)
                        sp.dma_start(ring[:, e0(u):e0(u) + 2, 0:CHUNK], pair_of(e0_d, q, u).rearrange(
                            "c (a n) -> c a n", a=2)).then_inc(e0_in[u // 2], 16)

                skewed(sp, [(2, load_x), (5, load_e0)])

                stored = sp.snap(b * (STEPS // 4 * 16) + 16)
                done(sp, q_done, b, 0, 0)
                for s in y_stored:
                    sp.wait_ge(s, stored)

                def stage_q(q, u):
                    if isinstance(q, int) and 4 * q + u == 1:
                        all_done(sp, q_done, b)
                    if not (isinstance(q, int) and 4 * q + u < 2):
                        done(sp, read_made, b, q, u, 2)
                    sp.dma_start(four(flat(q_in(u))), chunk_rows(plane_a, chunk_of(q, u))).then_inc(q_staged[u % 2], 16)

                def store_x1(q, u):
                    done(sp, x1_done, b, q, u)
                    sp.dma_start(x1_d[chunk_of(q, u)], flat(x1_out(u))).then_inc(x1_stored[u % 2], 16)

                def save_x1_t(q, u):
                    done(sp, x1_t_done, b, q, u)
                    sp.dma_start(chunk_rows(plane_b, place_of(q, u)), four(flat(x1_t(u)))).then_inc(x1_t_saved[u % 2], 16)

                skewed(sp, [(0, stage_q), (3, store_x1), (5, save_x1_t)])

                whole = sp.snap(b * STEPS + (STEPS + CREDIT))
                spectrum_read = sp.snap((b + 1) * (STEPS // 2 * 16) + 16)
                following = sp.snap((b + 1) % B)
                all_moved(sp, x1_stored, b)
                sp.wait_ge(cols_made, whole)

                def load_x1(q, u):
                    if not (isinstance(q, int) and 4 * q + u < 4):
                        done(sp, v_made, b, q, u, 4)
                    sp.dma_start(flat(x1_in(u)), x1_d[q * UNROLL + u]).then_inc(x1_loaded[u % 4], 16)

                def reload_x1(q, u):
                    if not (isinstance(q, int) and 4 * q + u < 2):
                        done(sp, base_done, b, q, u, 2)
                    sp.dma_start(flat(x1_again(u)), x1_d[q * UNROLL + u]).then_inc(x1_reloaded[u % 2], 16)

                def stage_y(q, u):
                    if isinstance(q, int) and 4 * q + u < 2:
                        sp.wait_ge(back_done, whole)
                    else:
                        done(sp, outf_turned, b, q, u, 2)
                    sp.dma_start(four(flat(y_in(u))), rows_of(plane_b, q, u)).then_inc(y_staged[u % 2], 16)

                def load_next(q, u):
                    if isinstance(q, int) and 4 * q + u == STEPS - 4:
                        for s in y_staged:
                            sp.wait_ge(s, spectrum_read)
                        load_first(following)

                def store_y(q, u):
                    done(sp, y_done, b, q, u)
                    if isinstance(q, int) and 4 * q + u == 0:
                        sp.nop(nofuse=True)
                    sp.dma_start(image_rows(out, b, q, u), flat(y_out(u))).then_inc(y_stored[u % 4], 16)

                skewed(sp, [(0, load_x1), (4, stage_y), (6, reload_x1), (9, load_next), (10, store_y)])
            all_moved(sp, y_stored, B - 1)
            for s in x_in + e0_in:
                sp.wait_ge(s, (B * (PAIRS // 2) + 2) * 16)

        @block.tensor
        def _(pe):
            mm = nc.tensor.matmul
            credit(pe, [e0_made, centered, normed, kv_made, q_made, ctx_added, read_made, turned, projected,
                        x1_turned, gram_added, ff1_made, s_made, cols_made, rows_made, back_made, v_made,
                        outf_turned, outf_made, out_s_made, gate_f_made])
            pe.wait_ge(loads, 16 * n_setup)
            for i in range(len(WEIGHTS)):
                last = nc.tensor.transpose(bank[:, i // 4, (i % 4) * 128:(i % 4 + 1) * 128], nat[:, i, :], square("ident"))
            last.then_inc(pe_ready, 1)
            pe.wait_ge(dve_ready, 3)
            nc.tensor.transpose(bank[0:MAPS, 4, 0:128], tap_maps_w[:, :], square("ident")).then_inc(pe_ready, 1)
            mm(bank[:, 5, 0:1], head_of[:, :], scale8[:, :], start=True, stop=True).then_inc(pe_ready, 1)
            mm(bank[:, 6, 0:128], nat[:, WEIGHTS.index("proj_f"), :], weight("gate_fs"),
               start=True, stop=True).then_inc(pe_ready, 1)
            pe.wait_ge(dve_ready, 4)

            def make_e0(q, u):
                done(pe, e0_copied, 0, q, u, 2)
                mm(bank[:, u % 2, :], tap_maps_t[:, :], maps[:, bass.ds(q * (UNROLL * CHUNK) + u * CHUNK, CHUNK)],
                   start=True, stop=True).then_inc(e0_made, 1)

            skewed(pe, [(0, make_e0)])
            pe.wait_ge(dve_ready, 6)

            with pe.Fori(0, B) as b:
                def center(q, u):
                    pair_done(pe, conv0, b, q, u)
                    done(pe, normed_t, b, q, u, 2)
                    for k in range(4):
                        last = mm(bank[:, u % 2, k * 128:(k + 1) * 128], flat(part(u))[:, k * 128:(k + 1) * 128],
                                  square("center"), start=True, stop=True)
                    last.then_inc(centered, 1)

                def turn_normed(q, u):
                    done(pe, normed_t, b, q, u)
                    done(pe, scaled, b, q, u, 1)
                    for k in range(4):
                        last = nc.tensor.transpose(bank[:, 2, k * 128:(k + 1) * 128],
                                                   flat(xhat_t(u))[:, k * 128:(k + 1) * 128], square("ident"))
                    last.then_inc(normed, 1)

                def make_kv(q, u):
                    done(pe, scaled, b, q, u)
                    done(pe, k_done, b, q, u, 1)
                    done(pe, v_done, b, q, u, 1)
                    for k in range(4):
                        last = mm(bank[:, 3 + k // 2, (k % 2) * 256:(k % 2 + 1) * 256],
                                  flat(xf(u))[:, k * 128:(k + 1) * 128],
                                  weights[:, 1:3, :].rearrange("p a n -> p (a n)"), start=True, stop=True)
                    last.then_inc(kv_made, 1)

                def make_q(q, u):
                    done(pe, q_done, b, q, u, 1)
                    mm(bank[:, 5, :], weight("q0"), flat(xf(u)), start=True, stop=True).then_inc(q_made, 1)

                def add_context(q, u):
                    done(pe, k_done, b, q, u)
                    done(pe, v_done, b, q, u)
                    for k in range(4):
                        last = mm(bank[:, 6, 0:129], blocks(k_t(u))[:, k, :], v_t[:, u % 2, k, :],
                                  start=False, stop=False)
                    last.then_inc(ctx_added, 1)

                pe.wait_ge(gate_f_done, b * STEPS + CREDIT)
                pe.wait_ge(gated, b * STEPS + CREDIT)
                mm(bank[:, 6, 0:129], zeros[:, 0:128], zeros[:, 0:129], start=True, stop=False)
                skewed(pe, [(2, turn_normed), (3, make_kv), (3, make_q), (0, center), (4, add_context)])
                mm(bank[:, 6, 0:129], zeros[:, 0:128], zeros[:, 0:129], start=False, stop=True).then_inc(small_pe, 1)

                all_done(pe, q_done, b)
                pe.wait_ge(small_dve, b * 8 + 1)

                def read_out(q, u):
                    moved(pe, q_staged, b, q, u)
                    done(pe, divided, b, q, u, 1)
                    for k in range(4):
                        last = mm(bank[:, k // 2, (k % 2) * 256:(k % 2) * 256 + 136],
                                  flat(q_in(u))[:, k * 128:(k + 1) * 128], read[:, :], start=True, stop=True)
                    last.then_inc(read_made, 1)

                def turn_out(q, u):
                    done(pe, divided, b, q, u)
                    done(pe, out_done, b, q, u, 1)
                    for k in range(4):
                        last = nc.tensor.transpose(bank[:, 2, k * 128:(k + 1) * 128],
                                                   flat(out_t(u))[:, k * 128:(k + 1) * 128], square("ident"))
                    last.then_inc(turned, 1)

                def project(q, u):
                    done(pe, out_done, b, q, u)
                    done(pe, x1_done, b, q, u, 1)
                    mm(bank[:, 3, :], weight("proj0"), flat(out_c(u)), start=True, stop=True).then_inc(projected, 1)

                def turn_x1(q, u):
                    done(pe, x1_done, b, q, u)
                    done(pe, x1_t_done, b, q, u, 1)
                    for k in range(4):
                        to = in_place(u, k)
                        last = nc.tensor.transpose(bank[:, 4, to * 128:(to + 1) * 128],
                                                   flat(x1_out(u))[:, k * 128:(k + 1) * 128], square("ident"))
                    last.then_inc(x1_turned, 1)

                def make_ff1(q, u):
                    done(pe, gelu_done, b, q, u, 1)
                    mm(bank[:, 5, :], weight("ff1"), flat(x1_out(u)), start=True, stop=True).then_inc(ff1_made, 1)

                def add_gram(q, u):
                    done(pe, x1_t_done, b, q, u)
                    for k in range(4):
                        y = flat(x1_t(u))[:, k * 128:(k + 1) * 128]
                        last = mm(bank[:, 7, 0:128], y, y, start=False, stop=False)
                    last.then_inc(gram_added, 1)

                def make_s(q, u):
                    done(pe, gelu_done, b, q, u)
                    done(pe, s_done, b, q, u, 1)
                    for k in range(4):
                        to = in_place(u, k)
                        last = mm(bank[:, 6, to * 128:(to + 1) * 128], flat(gelu(u))[:, k * 128:(k + 1) * 128],
                                  weight("ff2"), start=True, stop=True)
                    last.then_inc(s_made, 1)

                mm(bank[:, 7, 0:128], zeros[:, 0:128], zeros[:, 0:128], start=True, stop=False)
                skewed(pe, [(0, read_out), (1, turn_out), (2, project), (3, turn_x1), (3, make_ff1),
                            (4, add_gram), (4, make_s)])
                mm(bank[:, 7, 0:128], zeros[:, 0:128], zeros[:, 0:128], start=False, stop=True).then_inc(small_pe, 1)
                all_done(pe, s_done, b)

                def columns(q, u):
                    done(pe, folded_x, b, q, u)
                    done(pe, folded_s, b, q, u)
                    done(pe, split_x, b, q, u, 1)
                    done(pe, split_s, b, q, u, 1)
                    for i, slot in enumerate((fold_x(u), fold_s(u))):
                        for k in range(4):
                            last = mm(bank[:, i, k * 128:(k + 1) * 128], flat(slot)[:, k * 128:(k + 1) * 128],
                                      square("col_fwd"), start=True, stop=True)
                    last.then_inc(cols_made, 1)

                def rows(q, u):
                    done(pe, split_x, b, q, u)
                    done(pe, split_s, b, q, u)
                    done(pe, products, b, q, u, 1)
                    for i, (slot, m) in enumerate(((t1x(u), "row_even"), (t2x(u), "row_mix"),
                                                   (t1s(u), "row_even"), (t2s(u), "row_mix"))):
                        last = mm(bank[:, 2 + i, 0:4 * KW], square(m), ring[:, slot, 0:4 * KW], start=True, stop=True)
                    last.then_inc(rows_made, 1)

                def rows_back(q, u):
                    done(pe, packed, b, q, u)
                    done(pe, back_done, b, q, u, 1)
                    for k in range(4):
                        o = bank[:, 6, k * 128:(k + 1) * 128]
                        mm(o, flat(left(u, 0))[:, k * 128:(k + 1) * 128], square("row_cos"), start=True, stop=False)
                        last = mm(o, flat(left(u, 1))[:, k * 128:(k + 1) * 128], square("row_sin"),
                                  start=False, stop=True)
                    last.then_inc(back_made, 1)

                def score(q, u):
                    if isinstance(q, int) and 4 * q + u == 1:
                        pe.wait_ge(small_dve, b * 8 + 2)
                        mm(bank[:, 7, 0:128], gram[:, :], weight("k1"), start=True, stop=True).then_inc(small_pe, 1)
                    if isinstance(q, int) and 4 * q + u == 2:
                        pe.wait_ge(small_dve, b * 8 + 3)
                        mm(bank[:, 7, 0:128], weight("q1"), gram_k[:, :], start=True, stop=True).then_inc(small_pe, 1)

                skewed(pe, [(0, columns), (0, score), (1, rows), (3, rows_back)])

                pe.wait_ge(small_dve, b * 8 + 7)
                mm(bank[:, 7, 0:128], attn[:, :], weight("proj_s"), start=True, stop=True).then_inc(small_pe, 1)

                def make_v(q, u):
                    moved(pe, x1_loaded, b, q, u)
                    done(pe, v_saved, b, q, u, 1)
                    mm(bank[:, 0, :], weight("v1"), flat(x1_in(u)), start=True, stop=True).then_inc(v_made, 1)

                def columns_back(q, u):
                    moved(pe, y_staged, b, q, u)
                    done(pe, outf_copied, b, q, u, 1)
                    for k in range(4):
                        last = mm(bank[:, 1, k * 128:(k + 1) * 128], flat(y_in(u))[:, k * 128:(k + 1) * 128],
                                  square("col_inv"), start=True, stop=True)
                    last.then_inc(outf_turned, 1)

                def project_f(q, u):
                    done(pe, outf_copied, b, q, u)
                    done(pe, gated, b, q, u, 2)
                    done(pe, gate_s_done, b, q, u, 1)
                    mm(bank[:, 2 + u % 2, :], weight("proj_f"), flat(outf_in(u)), start=True, stop=True)
                    mm(bank[:, 4, :], weight("gate_fs"), flat(outf_in(u)), start=True, stop=True).then_inc(outf_made, 1)

                def project_s(q, u):
                    if isinstance(q, int) and 4 * q + u == 0:
                        pe.wait_ge(small_dve, b * 8 + 8)
                    pair_done(pe, conv1, b, q, u)
                    done(pe, out_s_done, b, q, u, 1)
                    mm(four(bank[:, 5, :]), mix[:, :], rows_of(plane_a, q, u), start=True, stop=False)
                    mm(bank[:, 5, :], weight("proj_s"), flat(conv_v(u)), start=False, stop=True).then_inc(out_s_made, 1)

                def make_gate_f(q, u):
                    done(pe, out_s_done, b, q, u)
                    done(pe, gate_f_done, b, q, u, 1)
                    mm(bank[:, 6, :], weight("gate_sf"), flat(out_s(u)), start=True, stop=True).then_inc(gate_f_made, 1)

                skewed(pe, [(0, make_v), (5, columns_back), (6, make_gate_f), (6, project_f), (5, project_s)])

        @block.scalar
        def _(act):
            op = nc.scalar.activation
            credit(act, [last_taps, last_taps_v, e0_copied, squared, scaled, k_done, v_done, q_done, out_done, x1_t_done, gelu_done, split_x,
                         spec_done, back_done, v_saved, outf_copied, gate_s_done, out_s_done, gate_f_done])

            def copy_e0(q, u):
                done(act, e0_made, 0, q, u)
                moved(act, e0_out, 0, q, u, 2)
                op(flat(part(u)), bank[:, u % 2, :], ACT.Copy).then_inc(e0_copied, 1)

            for q in range(QUADS):
                for u in range(UNROLL):
                    copy_e0(q, u)
            act.wait_ge(dve_ready, 6)

            with act.Fori(0, B) as b:
                def make_last_taps(q, u):
                    if u % 2 == 0:
                        pair_moved(act, x_in, b, q, u)
                    done(act, seeded, b, q, u, 4)
                    op(four(flat(tap_a(u))), tap_rows(plane_b, q, u, TAPS - 2), ACT.Copy, scale=taps0[:, TAPS - 2:TAPS - 1])
                    op(four(flat(tap_b(u))), tap_rows(plane_b, q, u, TAPS - 1), ACT.Copy,
                       scale=taps0[:, TAPS - 1:TAPS]).then_inc(last_taps, 1)

                def square_up(q, u):
                    done(act, centered, b, q, u)
                    done(act, normed_t, b, q, u, 2)
                    for k in range(4):
                        last = op(ring[:, junk, k * 128:(k + 1) * 128], bank[:, u % 2, k * 128:(k + 1) * 128],
                                  ACT.Square, accum_out=sumsq[:, u % 2, k:k + 1])
                    last.then_inc(ln_chain, 1)
                    act.wait_ge(ln_chain, b * STEPS + q * UNROLL + (u + 1))
                    op(std[:, u % 2, :], sumsq[:, u % 2, :], ACT.Sqrt, bias=eps[:, :], scale=1.0 / C).then_inc(squared, 1)

                def scale_shift(q, u):
                    done(act, normed, b, q, u)
                    done(act, kv_made, b, q, u, 2)
                    done(act, q_made, b, q, u, 2)
                    op(flat(xf(u)), bank[:, 2, :], ACT.Identity, bias=vector("ln_b"), scale=vector("ln_g")).then_inc(scaled, 1)

                def finish_kv(q, u):
                    done(act, kv_made, b, q, u)
                    done(act, ctx_added, b, q, u, 2)
                    kv = bank[:, 3:5, :].rearrange("p a (k n) -> p (a k) n", n=256)
                    op(blocks(k_t(u)), kv[:, :, 0:128], ACT.Relu).then_inc(k_done, 1)
                    op(v_t[:, u % 2, :, 0:128], kv[:, :, 128:256], ACT.Copy).then_inc(v_done, 1)

                def finish_q(q, u):
                    done(act, q_made, b, q, u)
                    op(rows_of(plane_a, q, u), four(bank[:, 5, :]), ACT.Relu).then_inc(q_done, 1)

                skewed(act, [(9, scale_shift), (10, finish_kv), (10, finish_q), (7, square_up), (2, make_last_taps)])

                def copy_out(q, u):
                    done(act, turned, b, q, u)
                    done(act, projected, b, q, u, 2)
                    op(flat(out_c(u)), bank[:, 2, :], ACT.Copy).then_inc(out_done, 1)

                def copy_x1_t(q, u):
                    done(act, x1_turned, b, q, u)
                    done(act, gram_added, b, q, u, 2)
                    moved(act, x1_t_saved, b, q, u, 2)
                    op(flat(x1_t(u)), bank[:, 4, :], ACT.Copy).then_inc(x1_t_done, 1)

                def make_gelu(q, u):
                    done(act, ff1_made, b, q, u)
                    done(act, s_made, b, q, u, 2)
                    op(flat(gelu(u)), bank[:, 5, :], ACT.Gelu).then_inc(gelu_done, 1)

                skewed(act, [(1, copy_out), (3, copy_x1_t), (3, make_gelu)])

                def exponents(q, u):
                    if isinstance(q, int) and 4 * q + u == 3:
                        act.wait_ge(small_dve, b * 8 + 5)
                        op(probs[:, :], scores[:, :], ACT.Exp, bias=peak[:, :], accum_out=total[:, :]).then_inc(small_act, 1)

                def split(q, u):
                    done(act, cols_made, b, q, u)
                    done(act, rows_made, b, q, u, 2)
                    cols = bank[:, 0, :].rearrange("p (k n) -> p k n", n=128)
                    re, im = slice(0, KW), slice(KW, 128)
                    one, two = blocks(t1x(u), KW), blocks(t2x(u), KW)
                    op(one[0:HALF, :, :], cols[0:HALF, :, re], ACT.Copy)
                    op(one[HALF:128, :, 1:KW - 1], cols[HALF:128, :, im], ACT.Copy)
                    op(two[0:HALF, :, 1:KW - 1], cols[0:HALF, :, im], ACT.Copy)
                    op(two[HALF:128, :, :], cols[HALF:128, :, re], ACT.Copy).then_inc(split_x, 1)

                def copy_spec(q, u):
                    done(act, rows_made, b, q, u)
                    done(act, products, b, q, u, 1)
                    op(ring[:, spec_x(0), 0:4 * KW], bank[:, 2, 0:4 * KW], ACT.Copy)
                    op(ring[:, spec_x(1), 0:4 * KW], bank[:, 3, 0:4 * KW], ACT.Copy).then_inc(spec_done, 1)

                def copy_back(q, u):
                    done(act, back_made, b, q, u)
                    group = plane_b[:, 1:H + 1, bass.ds(q * (UNROLL * GROUP) + (u * GROUP + 1), GROUP)]
                    op(group.rearrange("p h c -> p c h"), bank[:, 6, :].rearrange("p (k n) -> p k n", n=128),
                       ACT.Copy).then_inc(back_done, 1)

                skewed(act, [(0, exponents), (0, split), (1, copy_spec), (3, copy_back)])

                def save_v(q, u):
                    done(act, v_made, b, q, u)
                    op(rows_of(plane_a, q, u), four(bank[:, 0, :]), ACT.Copy).then_inc(v_saved, 1)

                def make_last_taps_v(q, u):
                    if isinstance(q, int) and 4 * q + u == STEPS - 1:
                        done(act, v_saved, b, q, u)
                    else:
                        done(act, v_saved, b, q, u, -1)
                    pair_done(act, conv1, b, q, u, 2)
                    done(act, seeded_v, b, q, u, 2)
                    op(four(flat(seed_v(u))), tap_rows(plane_a, q, u, TAPS - 2), ACT.Copy, scale=taps1[:, TAPS - 2:TAPS - 1])
                    op(four(flat(tap_v(u))), tap_rows(plane_a, q, u, TAPS - 1), ACT.Copy,
                       scale=taps1[:, TAPS - 1:TAPS]).then_inc(last_taps_v, 1)

                def copy_outf(q, u):
                    done(act, outf_turned, b, q, u)
                    done(act, outf_made, b, q, u, 2)
                    op(flat(outf_in(u)), bank[:, 1, :], ACT.Copy).then_inc(outf_copied, 1)

                def finish_gate_s(q, u):
                    done(act, outf_made, b, q, u)
                    done(act, base_done, b, q, u, 2)
                    op(flat(gate_s(u)), bank[:, 4, :], ACT.Sigmoid, bias=vector("b_gfs")).then_inc(gate_s_done, 1)

                def copy_out_s(q, u):
                    done(act, out_s_made, b, q, u)
                    done(act, gate_f_made, b, q, u, 2)
                    done(act, base_done, b, q, u, 2)
                    op(flat(out_s(u)), bank[:, 5, :], ACT.Copy).then_inc(out_s_done, 1)

                def finish_gate_f(q, u):
                    done(act, gate_f_made, b, q, u)
                    done(act, gated, b, q, u, 2)
                    op(flat(gate_f(u)), bank[:, 6, :], ACT.Sigmoid, bias=vector("b_gsf")).then_inc(gate_f_done, 1)

                skewed(act, [(0, save_v), (1, make_last_taps_v), (5, copy_outf), (6, finish_gate_f),
                             (6, finish_gate_s), (5, copy_out_s)])

        def fold(eng, plane, o, q, u):
            c = bass.ds(q * (UNROLL * GROUP) + (u * GROUP + 1), GROUP)
            low = plane[:, 1:HALF + 1, c].rearrange("p h c -> p c h")
            high = plane[:, HALF + 1:H + 1, c].rearrange("p h c -> p c h")
            eng.tensor_tensor(o[:, :, 0:HALF], low, high, ALU.add)
            return eng.tensor_tensor(o[:, :, HALF:128], low, high, ALU.subtract)

        @block.vector
        def _(dve):
            v = nc.vector
            credit(dve, [folded_x, conv0, normed_t, divided, x1_done, s_done, folded_s, split_s, products, conv1, gated, y_done])
            v.memset(zeros[:, :], 0.0)
            v.memset(eps[:, :], LN_EPS)
            for u in range(2):
                v.memset(v_t[:, u, :, 128:129], 1.0)
            dve.wait_ge(loads, 16 * n_setup)
            for p in range(2):
                v.tensor_scalar(tap_maps_w[:, 0:2 * TAPS].rearrange("p (t e) -> p t e", e=2)[:, :, p], taps0[:, :],
                                parity[:, p:p + 1], None, ALU.mult)
            v.tensor_copy(tap_maps_w[:, 2 * TAPS:MAPS], vector("conv_b")).then_inc(dve_ready, 1)
            dve.wait_ge(pe_ready, 1)
            v.tensor_copy(weights[:, 0:8, :], bank[:, 0:2, :].rearrange("p a (k n) -> p (a k) n", n=128)).then_inc(dve_ready, 1)
            v.tensor_copy(weights[:, 8:13, :], bank[:, 2:4, :].rearrange("p a (k n) -> p (a k) n", n=128)[:, 0:5, :]
                          ).then_inc(dve_ready, 1)
            dve.wait_ge(pe_ready, 4)
            v.tensor_copy(tap_maps_t[:, :], bank[0:MAPS, 4, 0:128]).then_inc(dve_ready, 1)
            v.tensor_copy(scale_col[:, :], bank[:, 5, 0:1])
            v.tensor_copy(weight("gate_fs"), bank[:, 6, 0:128]).then_inc(dve_ready, 1)
            all_done(dve, e0_copied, 0)
            for plane in (plane_a, plane_b):
                v.memset(plane[:, 0, :], 0.0)
                v.memset(plane[:, H + 1, :], 0.0)
                v.memset(plane[:, 1:H + 1, 0:1], 0.0)
                last = v.memset(plane[:, 1:H + 1, W + 1:W + 2], 0.0)
            last.then_inc(dve_ready, 1)

            def conv(plane, taps, slots, seeds, seen, finished, share):
                for t in share:
                    for i in range(2):
                        o = four(flat(slots[i]))
                        if t:
                            dve.wait_ge(dve_chain, seen + (2 * (t - 1) + i + 1))
                        ins = v.scalar_tensor_tensor(out=o, in0=plane(i, t), scalar=taps[:, t:t + 1],
                                                     in1=o if t else four(flat(seeds[i])), op0=ALU.mult, op1=ALU.add)
                        ins.then_inc(finished if t == DVE_TAPS - 1 and i else dve_chain, 1)

            def share_of(w):
                return range(FIRST_TAPS, DVE_TAPS) if w % 2 else range(FIRST_TAPS)

            CHAIN = 2 * DVE_TAPS - 1

            with dve.Fori(0, B) as b:
                def conv_x(q, w):
                    u = w // 2 * 2
                    if w == u:
                        done(dve, seeded, b, q, u, -1)
                        done(dve, centered, b, q, u, 3)
                    seen = b * (2 * PAIRS * CHAIN) + q * (UNROLL // 2 * CHAIN) + u // 2 * CHAIN
                    conv(lambda i, t: tap_rows(plane_b, q, u + i, t), taps0, (part(u), part(u + 1)),
                         (seeds(u), seeds(u + 1)), seen, conv0, share_of(w))

                def normalize(q, u):
                    done(dve, squared, b, q, u)
                    v.reciprocal(rstd[:, u % 2, :], std[:, u % 2, :]).then_inc(small_chain, 1)
                    dve.wait_ge(small_chain, b * (3 * STEPS) + q * UNROLL + (u + 1))
                    done(dve, normed, b, q, u, 2)
                    v.tensor_tensor(blocks(xhat_t(u)), bank[:, u % 2, :].rearrange("p (k n) -> p k n", n=128),
                                    rstd[:, u % 2, :].unsqueeze(2).broadcast_to([128, 4, 128]), ALU.mult).then_inc(normed_t, 1)

                skewed(dve, [(0, conv_x), (2, normalize)])
                dve.wait_ge(small_pe, b * 5 + 1)
                v.tensor_tensor(read[:, 0:128], bank[:, 6, 0:128], square("head_mask"), ALU.mult)
                v.tensor_copy(ksum[:, :], bank[:, 6, 128:129]).then_inc(ksum_done, 1)
                dve.wait_ge(ksum_done, b + 1)
                v.tensor_scalar(read[:, 128:136], head_cols, ksum[:, :], None, ALU.mult).then_inc(small_dve, 1)

                def divide(q, u):
                    done(dve, read_made, b, q, u)
                    n = bank[:, 0:2, :].rearrange("p a (k n) -> p (a k) n", n=256)
                    d = den[:, u % 2, :].rearrange("p (k h) -> p k h", h=HEADS)
                    v.tensor_scalar(d, n[:, :, 128:136], DEN_MIN, None, ALU.max).then_inc(small_chain, 1)
                    dve.wait_ge(small_chain, b * (3 * STEPS) + q * (2 * UNROLL) + (STEPS + 2 * u + 1))
                    v.reciprocal(rden[:, u % 2, :], den[:, u % 2, :]).then_inc(small_chain, 1)
                    dve.wait_ge(small_chain, b * (3 * STEPS) + q * (2 * UNROLL) + (STEPS + 2 * u + 2))
                    done(dve, turned, b, q, u, 2)
                    r = rden[:, u % 2, :].rearrange("p (k h) -> p k h", h=HEADS)
                    v.tensor_tensor(blocks(out_t(u)).rearrange("p k (h d) -> p k h d", d=HEAD),
                                    n[:, :, 0:128].rearrange("p k (h d) -> p k h d", d=HEAD),
                                    r.unsqueeze(3).broadcast_to([128, 4, HEADS, HEAD]), ALU.mult).then_inc(divided, 1)

                def add_x(q, u):
                    done(dve, projected, b, q, u)
                    done(dve, ff1_made, b, q, u, 2)
                    done(dve, x1_turned, b, q, u, 2)
                    moved(dve, x1_stored, b, q, u, 2)
                    v.scalar_tensor_tensor(out=four(flat(x1_out(u))), in0=four(bank[:, 3, :]), scalar=vector("proj_b"),
                                           in1=chunk_rows(plane_b, chunk_of(q, u)), op0=ALU.add, op1=ALU.add).then_inc(x1_done, 1)

                def save_s(q, u):
                    done(dve, s_made, b, q, u)
                    if u == 1:
                        moved(dve, q_staged, b, q, u, -2)
                    v.tensor_copy(chunk_rows(plane_a, place_of(q, u)), four(bank[:, 6, :])).then_inc(s_done, 1)

                skewed(dve, [(0, divide), (2, add_x), (4, save_s)])

                all_done(dve, s_done, b)
                all_done(dve, gram_added, b)
                all_done(dve, s_made, b)
                all_moved(dve, x1_t_saved, b)
                all_moved(dve, x1_stored, b)

                def softmax(q, u):
                    if not (isinstance(q, int) and q == 0):
                        return
                    if u == 0:
                        dve.wait_ge(small_pe, b * 5 + 2)
                        v.tensor_copy(gram[:, :], bank[:, 7, 0:128]).then_inc(small_dve, 1)
                    if u == 1:
                        dve.wait_ge(small_pe, b * 5 + 3)
                        v.tensor_copy(gram_k[:, :], bank[:, 7, 0:128]).then_inc(small_dve, 1)
                    if u == 2:
                        dve.wait_ge(small_pe, b * 5 + 4)
                        v.scalar_tensor_tensor(out=scores[:, :], in0=bank[:, 7, 0:128], scalar=scale_col[:, :],
                                               in1=square("head_off"), op0=ALU.mult, op1=ALU.add).then_inc(small_dve, 1)
                        dve.wait_ge(small_dve, b * 8 + 4)
                        v.tensor_reduce(peak[:, :], scores[:, :], mybir.AxisListType.X, ALU.max, negate=True).then_inc(small_dve, 1)
                    if u == 3:
                        dve.wait_ge(small_act, b + 1)
                        v.reciprocal(rtotal[:, :], total[:, :]).then_inc(small_dve, 1)
                        dve.wait_ge(small_dve, b * 8 + 6)
                        v.tensor_scalar(attn[:, :], probs[:, :], rtotal[:, :], None, ALU.mult).then_inc(small_dve, 1)

                def clear_edges():
                    for u in range(2):
                        for one, two in ((t1x(u), t2x(u)), (t1s(u), t2s(u))):
                            v.memset(blocks(one, KW)[HALF:128, :, 0:KW:KW - 1], 0.0)
                            last = v.memset(blocks(two, KW)[0:HALF, :, 0:KW:KW - 1], 0.0)
                    last.then_inc(edges_clear, 1)

                clear_edges()

                def fold_up(q, u):
                    done(dve, cols_made, b, q, u, 2)
                    fold(v, plane_b, blocks(fold_x(u)), q, u).then_inc(folded_x, 1)
                    fold(v, plane_a, blocks(fold_s(u)), q, u).then_inc(folded_s, 1)

                def split_up_s(q, u):
                    done(dve, cols_made, b, q, u)
                    done(dve, rows_made, b, q, u, 2)
                    cols = bank[:, 1, :].rearrange("p (k n) -> p k n", n=128)
                    re, im = slice(0, KW), slice(KW, 128)
                    one, two = blocks(t1s(u), KW), blocks(t2s(u), KW)
                    v.tensor_copy(one[0:HALF, :, :], cols[0:HALF, :, re])
                    v.tensor_copy(one[HALF:128, :, 1:KW - 1], cols[HALF:128, :, im])
                    v.tensor_copy(two[0:HALF, :, 1:KW - 1], cols[0:HALF, :, im])
                    v.tensor_copy(two[HALF:128, :, :], cols[HALF:128, :, re]).then_inc(split_s, 1)

                def multiply(q, u):
                    done(dve, spec_done, b, q, u)
                    done(dve, packed, b, q, u, 2)
                    for i, (xs, ss) in enumerate(((0, 4), (1, 5), (0, 5), (1, 4))):
                        last = v.tensor_tensor(ring[:, prod(u, i), 0:4 * KW], ring[:, spec_x(xs), 0:4 * KW],
                                               bank[:, ss, 0:4 * KW], ALU.mult)
                    last.then_inc(products, 1)

                skewed(dve, [(1, split_up_s), (0, fold_up), (2, multiply), (0, softmax)])

                dve.wait_ge(small_pe, b * 5 + 5)
                v.tensor_copy(mix[:, :], bank[:, 7, 0:128]).then_inc(small_dve, 1)
                all_done(dve, products, b)

                def conv_of_v(q, w):
                    u = w // 2 * 2
                    if w == u:
                        done(dve, seeded_v, b, q, u, -1)
                        done(dve, out_s_made, b, q, u, 3)
                    seen = b * (2 * PAIRS * CHAIN) + q * (UNROLL // 2 * CHAIN) + (u // 2 * CHAIN + PAIRS * CHAIN)
                    conv(lambda i, t: tap_rows(plane_a, q, u + i, t), taps1, (conv_v(u), conv_v(u + 1)),
                         (seed_v(u), seed_v(u + 1)), seen, conv1, share_of(w))

                def gate_out_f(q, u):
                    done(dve, gate_f_done, b, q, u)
                    done(dve, outf_made, b, q, u)
                    moved(dve, y_stored, b, q, u, 4)
                    v.tensor_tensor(flat(y_out(u)), bank[:, 2 + u % 2, :], flat(gate_f(u)), ALU.mult).then_inc(gated, 1)

                def finish(q, u):
                    done(dve, gated, b, q, u)
                    done(dve, base_done, b, q, u)
                    v.tensor_tensor(flat(y_out(u)), flat(y_out(u)), flat(base(u)), ALU.add).then_inc(y_done, 1)

                skewed(dve, [(3, conv_of_v), (7, gate_out_f), (7, finish)])

        @block.gpsimd
        def _(pool):
            g = nc.gpsimd
            credit(pool, [seeded, seeded_v, packed, base_done])
            with pool.Fori(0, B) as b:
                pool.wait_ge(base_done, b * STEPS + CREDIT)

                def seed(q, u):
                    done(pool, last_taps, b, q, u)
                    pair_moved(pool, e0_in, b, q, u)
                    pair_done(pool, conv0, b, q, u, 2)
                    g.tensor_tensor(flat(seeds(u)), flat(e0(u)), flat(tap_a(u)), ALU.add).then_inc(seed_chain, 1)
                    pool.wait_ge(seed_chain, b * STEPS + q * UNROLL + (u + 1))
                    g.tensor_tensor(flat(seeds(u)), flat(seeds(u)), flat(tap_b(u)), ALU.add).then_inc(seeded, 1)

                skewed(pool, [(1, seed)])

                def pack(q, u):
                    done(pool, products, b, q, u)
                    done(pool, back_made, b, q, u, 2)
                    rr, ii, ri, ir = (blocks(prod(u, i), KW) for i in range(4))
                    one, two = blocks(left(u, 0)), blocks(left(u, 1))
                    mid = slice(1, KW - 1)
                    g.tensor_tensor(one[:, :, 0:KW], rr, ii, ALU.subtract)
                    g.tensor_tensor(one[:, :, KW:128], ri[:, :, mid], ir[:, :, mid], ALU.add)
                    g.tensor_tensor(two[:, :, 0:KW], ri, ir, ALU.add)
                    g.tensor_tensor(two[:, :, KW:128], ii[:, :, mid], rr[:, :, mid], ALU.subtract).then_inc(packed, 1)

                skewed(pool, [(0, pack)])

                def gate_out_s(q, u):
                    done(pool, gate_s_done, b, q, u)
                    done(pool, out_s_done, b, q, u)
                    done(pool, y_done, b, q, u, 2)
                    g.tensor_tensor(flat(base(u)), flat(out_s(u)), flat(gate_s(u)), ALU.mult).then_inc(pool_chain, 1)
                    pool.wait_ge(pool_chain, b * STEPS + q * UNROLL + (u + 1))
                    moved(pool, x1_reloaded, b, q, u)
                    g.tensor_tensor(flat(base(u)), flat(base(u)), flat(x1_again(u)), ALU.add).then_inc(base_done, 1)

                def seed_of_v(q, u):
                    done(pool, last_taps_v, b, q, u)
                    g.tensor_tensor(flat(seed_v(u)), flat(seed_v(u)), flat(tap_v(u)), ALU.add).then_inc(seeded_v, 1)

                skewed(pool, [(1, seed_of_v), (6, gate_out_s)])


_ARGS = {
    "proj_b": "L0_conv_proj_b", "conv_b": "L0_conv_conv_b", "ln_g": "L0_conv_ln_g", "ln_b": "L0_conv_ln_b",
    "b_gsf": "L1_conv_b_gsf", "b_gfs": "L1_conv_b_gfs", "scale_s": "L1_conv_scale_s",
    "conv_w": "L0_conv_conv_w", "W_dw": "L1_conv_W_dw", "proj0": "L0_conv_proj_w", "proj_s": "L1_conv_W_proj_s",
    "ff1": "L1_conv_W_ff1", "ff2": "L1_conv_W_ff2", "proj_f": "L1_conv_W_proj_f", "gate_sf": "L1_conv_W_gsf",
    "gate_fs": "L1_conv_W_gfs",
}


def kernel(**inputs):
    import concourse.bacc as bacc
    from concourse.bass_utils import run_bass_kernel_spmd

    nc = bacc.Bacc("TRN2", target_bir_lowering=False, num_devices=1, dynamic_dma_scratch_size=2048)
    arrays = {name: np.ascontiguousarray(a) for name, a in inputs.items()}
    arrays["x"] = arrays["x"].reshape(-1, C, PIX)
    arrays.update(shape_constants())
    aps = {name: nc.dram_tensor("in_" + name, a.shape, F32, kind="ExternalInput").ap() for name, a in arrays.items()}
    out = nc.dram_tensor("out", (B, C, PIX), F32, kind="ExternalOutput").ap()
    w = {short: aps[name] for short, name in _ARGS.items()}
    for i, part in enumerate("qkv"):
        w[f"{part}0"] = aps["L0_conv_qkv_w"][i * C:(i + 1) * C, :]
        w[f"{part}1"] = aps["L1_conv_W_qkv"][i * C:(i + 1) * C, :]
    conv_seq_kernel(nc, aps["x"], w, aps["squares"], aps["parity"], aps["head_of"], aps["head_cols"], aps["maps"], out)
    result = run_bass_kernel_spmd(nc, [{"in_" + name: a for name, a in arrays.items()}], core_ids=[0])
    return result.results[0]["out"].reshape(B, C, H, W)
```

```python
from contextlib import ExitStack

import numpy as np

import concourse.bass as bass
from concourse import mybir

F32 = mybir.dt.float32
ALU = mybir.AluOpType
ACT = mybir.ActivationFunctionType

B, C, H, W = 8, 128, 128, 128
HEADS = 8
HEAD = C // HEADS
PIX = H * W
ROWS = 4
CHUNK = ROWS * W
STEPS = H // ROWS
GROUP = 4
UNROLL = 4
QUADS = STEPS // UNROLL
PAIRS = STEPS // 2
KW = W // 2 + 1
KI = W // 2 - 1
HALF = H // 2
PAD = W + 2
TAPS = 9
DVE_TAPS = (6, 7)
MAPS = 2 * TAPS + 1
CREDIT = 4

LN_EPS = 1e-5
DEN_MIN = 1e-6

SQUARES = ["ident", "center", "head_mask", "head_off", "col_fwd", "row_even", "row_mix", "row_cos", "row_sin", "col_inv"]
WEIGHTS = ["q0", "k0", "v0", "proj0", "q1", "k1", "v1", "proj_s", "ff1", "ff2", "proj_f", "gate_sf", "gate_fs"]
VECTORS = ["proj_b", "conv_b", "ln_g", "ln_b", "b_gsf", "b_gfs"]


def shape_constants():
    f = np.float64
    k = np.arange(128)
    head = k // HEAD
    same = head[:, None] == head[None, :]
    sq = {}
    sq["ident"] = np.eye(C)
    sq["center"] = np.eye(C) - 1.0 / C
    sq["head_mask"] = same
    sq["head_off"] = np.where(same, 0.0, -1e30)
    w, kr, ki = k[:, None].astype(f), np.arange(KW)[None, :], np.arange(1, KI + 1)[None, :]
    sq["col_fwd"] = np.concatenate([np.cos(2 * np.pi * w * kr / W), np.sin(2 * np.pi * w * ki / W)], 1)
    h = np.arange(HALF)[:, None] + 0.5
    cos, sin = np.cos(2 * np.pi * h * k[None, :] / H), np.sin(2 * np.pi * h * k[None, :] / H)
    sq["row_even"] = np.concatenate([cos, -sin], 0)
    sq["row_mix"] = np.concatenate([cos, sin], 0)
    sq["row_cos"] = np.cos(2 * np.pi * k[:, None] * (k[None, :] + 1) / H)
    sq["row_sin"] = np.sin(2 * np.pi * k[:, None] * (k[None, :] + 1) / H)
    scale = 1.0 / np.sqrt(float(PIX)) ** 3
    weight = np.where((kr == 0) | (kr == W // 2), 1.0, 2.0).T * scale
    wc = k[None, :].astype(f)
    sq["col_inv"] = np.concatenate([weight * np.cos(2 * np.pi * kr.T * wc / W),
                                    2 * scale * np.sin(2 * np.pi * ki.T * wc / W)], 0)
    squares = np.stack([sq[n] for n in SQUARES], 1).astype(np.float32)
    parity = np.stack([k % 2 == 0, k % 2 == 1], 1).astype(np.float32)
    head_of = (np.arange(HEADS)[:, None] == head[None, :]).astype(np.float32)
    yc = (np.arange(H, dtype=np.float32) - H // 2)[:, None]
    xc = (np.arange(W, dtype=np.float32) - W // 2)[None, :]
    rho = np.sqrt(xc ** 2 + yc ** 2) / np.float32(max(H, W) / 2)
    theta = (np.arctan2(yc + 0 * xc, xc + 0 * yc) + np.float32(np.pi)) / np.float32(2 * np.pi)
    padded = np.pad(np.stack([rho, theta]), ((0, 0), (1, 1), (1, 1)))
    maps = np.ones((MAPS, H, W), np.float32)
    for t in range(TAPS):
        maps[2 * t:2 * t + 2] = padded[:, t // 3:t // 3 + H, t % 3:t % 3 + W]
    return {"squares": squares, "parity": parity, "head_of": head_of, "head_cols": head_of.T.copy(),
            "maps": maps.reshape(MAPS, PIX)}


def skewed(eng, stages):
    deepest = max(lag for lag, _ in stages)
    first = -(-deepest // UNROLL)

    def turn(q, w):
        for lag, stage in stages:
            sq, su = q + (w - lag) // UNROLL, (w - lag) % UNROLL
            if isinstance(sq, int) and not 0 <= sq < QUADS:
                continue
            stage(sq, su)

    for q in range(first):
        for w in range(UNROLL):
            turn(q, w)
    with eng.Fori(0, QUADS - first) as p:
        for w in range(UNROLL):
            turn(p + first, w)
    for i in range(deepest):
        turn(QUADS + i // UNROLL, i % UNROLL)


def at_end(*calls):
    def stage(q, u):
        if isinstance(q, int) and 4 * q + u == STEPS - 1:
            for call in calls:
                call()
    return stage


def after(first, stage):
    def rest(q, u):
        if not (isinstance(q, int) and 4 * q + u < first):
            stage(q, u)
    return rest


def conv_seq_kernel(nc, x, w, squares_d, parity_d, head_of_d, head_cols_d, maps_d, out):
    ctx = ExitStack()
    with ctx:
        def sb(name, shape, dt=F32):
            return ctx.enter_context(nc.sbuf_tensor(name, shape, dt))

        def sem(name):
            return ctx.enter_context(nc.semaphore(name))

        plane_a = sb("plane_a", [128, H + 2, PAD])
        plane_b = sb("plane_b", [128, H + 2, PAD])
        squares = sb("squares", [128, len(SQUARES), 128])
        weights = sb("weights", [128, len(WEIGHTS), 128])
        ring = sb("ring", [128, 32, CHUNK])
        xhat = sb("xhat", [128, 4, 4, 129])
        parity = sb("parity", [128, 2])
        head_of = sb("head_of", [HEADS, 128])
        head_cols_t = sb("head_cols", [128, HEADS])
        scale8 = sb("scale8", [HEADS, 1])
        vectors = sb("vectors", [128, len(VECTORS)])
        taps0 = sb("taps0", [128, TAPS])
        taps1 = sb("taps1", [128, TAPS])
        tap_maps_w = sb("tap_maps_w", [128, MAPS])
        tap_maps_t = sb("tap_maps_t", [MAPS, 128])
        eps = sb("eps", [128, 1])
        zeros = sb("zeros", [128, 136])
        ksum = sb("ksum", [128, 1])
        read = sb("read", [128, 136])
        std = sb("std", [128, 2, 4])
        sumsq = sb("sumsq", [128, 2, 4])
        rstd = sb("rstd", [128, 2, 4])
        den = sb("den", [128, 2, 4 * HEADS])
        rden = sb("rden", [128, 2, 4 * HEADS])
        scale_col = sb("scale_col", [128, 1])
        shift_v = sb("shift_v", [128, 128])
        ctx_x = sb("ctx_x", [128, 128])
        ctx_t = sb("ctx_t", [128, 128])
        gram = scores = ctx_x
        gram_k = probs = ctx_t
        attn = sb("attn", [128, 128])
        peak = sb("peak", [128, 1])
        total = sb("total", [128, 1])
        rtotal = sb("rtotal", [128, 1])
        mix = sb("mix", [128, 128])
        bank = ctx.enter_context(nc.psum_tensor("bank", [128, 8, 512], F32))
        e0_d = nc.dram_tensor("e0_scratch", (128, PIX), F32, kind="Internal").ap()
        x1_d = nc.dram_tensor("x1_scratch", (STEPS, 128, CHUNK), F32, kind="Internal").ap()

        head_cols = head_cols_t[:, :]

        def square(name):
            return squares[:, SQUARES.index(name), :]

        def weight(name):
            return weights[:, WEIGHTS.index(name), :]

        def vector(name):
            i = VECTORS.index(name)
            return vectors[:, i:i + 1]

        def flat(slot):
            return ring[:, slot, 0:CHUNK]

        def blocks(slot, width=128):
            return ring[:, slot, 0:4 * width].rearrange("p (b n) -> p b n", n=width)

        def e0(u): return 0 + u % 4
        junk = 5
        def tap(u, i): return ((26, 27, 28), (29, 30, 31), (4, 6, 8), (7, 9, 16))[u % 4][i]
        def seeds(u): return (10, 11, 14, 15)[u % 4]
        def xf(u): return 18 + u % 2
        def k_t(u): return 20 + u % 2
        def part(u): return 22 + u % 4

        def x1_out(u): return 20 + u % 2
        def q_in(u): return 12 + u % 2
        def out_t(u): return 24 + u % 2
        def x1_t(u): return 26 + u % 2
        def out_c(u): return 28 + u % 2
        def gelu(u): return 30 + u % 2

        def fold_x(u): return 0 + u % 2
        def fold_s(u): return 2 + u % 2
        def t1x(u): return 4 + u % 2
        def t2x(u): return 6 + u % 2
        def t1s(u): return 8 + u % 2
        def t2s(u): return 10 + u % 2
        def spec_x(i): return 12 + i
        def prod(u, i): return 14 + 4 * (u % 2) + i
        def left(u, i): return 22 + 2 * (u % 2) + i

        def x1_in(u): return 26 + u % 4
        def x1_again(u): return 4 + u % 2
        def y_in(u): return 6 + u % 2
        def outf_in(u): return 8 + u % 2
        def conv_v(u): return 10 + u % 4
        def gate_s(u): return 14 + u % 2
        def out_s(u): return 16 + u % 2
        def gate_f(u): return 18 + u % 2
        def base(u): return 20 + u % 2
        def y_out(u): return 22 + u % 4
        def seed_v(u): return 0 + u % 4
        def tap_v(u): return 30 + u % 2

        def rows_of(plane, q, u):
            return plane[:, bass.ds(q * (UNROLL * ROWS) + (u * ROWS + 1), ROWS), 1:W + 1]

        def chunk_of(q, u):
            return (q * 2, q + 16, q * 2 + 1, q * -1 + 31)[u]

        def place_of(q, u):
            return (q * 2, q * -1 + 31, q * 2 + 1, q + 16)[u]

        def chunk_rows(plane, n):
            return plane[:, bass.ds(n * ROWS + 1, ROWS), 1:W + 1]

        def in_place(u, k):
            return 3 - k if u % 2 else k

        def tap_rows(plane, q, u, t):
            return plane[:, bass.ds(q * (UNROLL * ROWS) + (u * ROWS + t // 3), ROWS), t % 3:t % 3 + W]

        def load_piece(sp, b, q, u):
            piece = 4 * q + u if isinstance(q, int) else None
            above, below = int(piece != 0), int(piece != STEPS - 2)
            start, n = q * (UNROLL * ROWS) + (u * ROWS + above), 2 * ROWS - above + below
            sp.dma_start(plane_b[:, bass.ds(start + 1, n), 1:W + 1],
                         x[b].rearrange("c (h w) -> c h w", w=W)[:, bass.ds(start, n), :]).then_inc(x_in[u // 2], 16)

        def pair_of(ap, q, u):
            return ap.rearrange("c (n m) -> n c m", m=2 * CHUNK)[q * (UNROLL // 2) + u // 2]

        def image_rows(ap, b, q, u):
            return ap[b].rearrange("c (n m) -> n c m", m=CHUNK)[q * UNROLL + u]

        def four(ap):
            return ap.rearrange("p (r n) -> p r n", r=4)

        loads = sem("loads")
        dve_ready = sem("dve_ready")
        pe_ready = sem("pe_ready")
        stage_sems = {}

        def stage(name):
            stage_sems[name] = sem(name)
            return stage_sems[name]

        e0_made, e0_copied = stage("e0_made"), stage("e0_copied")
        last_taps = stage("last_taps")
        seeded = stage("seeded")
        conv0 = stage("conv0")
        centered = stage("centered")
        squared = stage("squared")
        normed_t = stage("normed_t")
        normed = stage("normed")
        scaled = stage("scaled")
        k_made = stage("k_made")
        k_done = stage("k_done")
        q_made = stage("q_made")
        q_done = stage("q_done")
        ctx_added = stage("ctx_added")
        read_made = stage("read_made")
        divided = stage("divided")
        turned = stage("turned")
        out_done = stage("out_done")
        projected = stage("projected")
        x1_done = stage("x1_done")
        x1_turned = stage("x1_turned")
        x1_t_done = stage("x1_t_done")
        gram_added = stage("gram_added")
        ff1_made = stage("ff1_made")
        gelu_done = stage("gelu_done")
        s_made = stage("s_made")
        s_done = stage("s_done")
        folded_x = stage("folded_x")
        folded_s = stage("folded_s")
        cols_made = stage("cols_made")
        split_x = stage("split_x")
        split_s = stage("split_s")
        rows_made = stage("rows_made")
        spec_done = stage("spec_done")
        products = stage("products")
        packed = stage("packed")
        back_made = stage("back_made")
        back_done = stage("back_done")
        v_made = stage("v_made")
        v_saved = stage("v_saved")
        last_taps_v = stage("last_taps_v")
        seeded_v = stage("seeded_v")
        conv1 = stage("conv1")
        outf_turned = stage("outf_turned")
        outf_copied = stage("outf_copied")
        outf_made = stage("outf_made")
        gate_s_done = stage("gate_s_done")
        out_s_made = stage("out_s_made")
        out_s_done = stage("out_s_done")
        gate_f_made = stage("gate_f_made")
        gate_f_done = stage("gate_f_done")
        base_done = stage("base_done")
        gated = stage("gated")
        y_done = stage("y_done")
        dve_chain = sem("dve_chain")
        ln_chain = sem("ln_chain")
        pool_chain = sem("pool_chain")
        seed_chain = sem("seed_chain")
        small_dve = sem("small_dve")
        small_act = sem("small_act")
        small_pe = sem("small_pe")
        small_chain = sem("small_chain")
        ksum_done = sem("ksum_done")
        maps_in = [sem(f"maps_in{i}") for i in range(8)]
        x_in = [sem(f"x_in{i}") for i in range(2)]
        e0_in = [sem(f"e0_in{i}") for i in range(2)]
        e0_out = [sem(f"e0_out{i}") for i in range(4)]
        q_staged = [sem(f"q_staged{i}") for i in range(2)]
        x1_stored = [sem(f"x1_stored{i}") for i in range(2)]
        x1_t_saved = [sem(f"x1_t_saved{i}") for i in range(2)]
        x1_loaded = [sem(f"x1_loaded{i}") for i in range(4)]
        x1_reloaded = [sem(f"x1_reloaded{i}") for i in range(2)]
        y_staged = [sem(f"y_staged{i}") for i in range(2)]
        y_stored = [sem(f"y_stored{i}") for i in range(4)]

        def done(eng, s, b, q, u, ago=0):
            eng.wait_ge(s, b * STEPS + q * UNROLL + (u + 1 + CREDIT - ago))

        def pair_done(eng, s, b, q, u, ago=0):
            eng.wait_ge(s, b * PAIRS + q * (UNROLL // 2) + (u // 2 + 1 + CREDIT - ago))

        def pair_moved(eng, sems, b, q, u, ago=0):
            n = u // 2 - ago
            eng.wait_ge(sems[n % 2], (b * (PAIRS // 2) + q + (n // 2 + 2)) * 16)

        def all_done(eng, s, b):
            eng.wait_ge(s, b * STEPS + (STEPS + CREDIT))

        def moved(eng, sems, b, q, u, ago=0):
            k = len(sems)
            n = u - ago
            eng.wait_ge(sems[n % k], (b * (STEPS // k) + q * (UNROLL // k) + (n // k + 2)) * 16)

        def all_moved(eng, sems, b):
            whole = (b + 1) * (STEPS // len(sems) * 16) + 16
            if not isinstance(b, int):
                whole = eng.snap(whole)
            for s in sems:
                eng.wait_ge(s, whole)

        def credit(eng, sems, count=CREDIT):
            for s in sems:
                eng.nop(nofuse=True).then_inc(s, count)

        block = ctx.enter_context(nc.Block())
        n_setup = 4 + len(VECTORS) + 3 + len(WEIGHTS)
        nat = plane_b[:, :, :].rearrange("p a b -> p (a b)")[:, 0:13 * 128].rearrange("p (a b) -> p a b", b=128)
        maps = plane_a[0:MAPS, :, :].rearrange("p a b -> p (a b)")

        @block.sync
        def _(sp):
            for sems in (x_in, e0_in, e0_out, q_staged, x1_stored, x1_t_saved, x1_loaded, x1_reloaded, y_staged, y_stored):
                credit(sp, sems, 16)
            sp.dma_start(squares[:, :, :], squares_d).then_inc(loads, 16)
            sp.dma_start(parity[:, :], parity_d).then_inc(loads, 16)
            sp.dma_start(head_of[:, :], head_of_d).then_inc(loads, 16)
            sp.dma_start(head_cols, head_cols_d).then_inc(loads, 16)
            for i, name in enumerate(VECTORS):
                sp.dma_start(vectors[:, i:i + 1], w[name].rearrange("(c o) -> c o", o=1)).then_inc(loads, 16)
            sp.dma_start(scale8[:, :], w["scale_s"].rearrange("h a b -> h (a b)")).then_inc(loads, 16)
            sp.dma_start(taps0[:, :], w["conv_w"].rearrange("c o a b -> c (o a b)")).then_inc(loads, 16)
            sp.dma_start(taps1[:, :], w["W_dw"].rearrange("c o a b -> c (o a b)")).then_inc(loads, 16)
            for i, name in enumerate(WEIGHTS):
                sp.dma_start(nat[:, i, :], w[name]).then_inc(loads, 16)
            for i, s in enumerate(maps_in):
                some = slice(i * (PIX // len(maps_in)), (i + 1) * (PIX // len(maps_in)))
                sp.dma_start(maps[:, some], maps_d[:, some]).then_inc(s, 16)

            def load_x_first(b):
                for u in (0, 2):
                    load_piece(sp, b, 0, u)

            def load_e0_first():
                for u in (0, 2):
                    sp.dma_start(ring[:, e0(u):e0(u) + 2, 0:CHUNK], pair_of(e0_d, 0, u).rearrange(
                        "c (a n) -> c a n", a=2)).then_inc(e0_in[u // 2], 16)

            sp.wait_ge(dve_ready, 6)
            load_x_first(0)

            def store_e0(q, u):
                done(sp, e0_copied, 0, q, u)
                sp.dma_start(e0_d.rearrange("c (n m) -> n c m", m=CHUNK)[q * UNROLL + u],
                             flat(part(u))).then_inc(e0_out[u % 4], 16)

            skewed(sp, [(0, store_e0)])
            all_moved(sp, e0_out, 0)
            load_e0_first()

            with sp.Fori(0, B) as b:
                def load_x(q, u):
                    if u % 2 == 0 and not (isinstance(q, int) and q == 0):
                        done(sp, last_taps, b, q, u, 4)
                        load_piece(sp, b, q, u)

                def load_e0(q, u):
                    if u % 2 == 0 and not (isinstance(q, int) and q == 0):
                        done(sp, seeded, b, q, u, 3)
                        sp.dma_start(ring[:, e0(u):e0(u) + 2, 0:CHUNK], pair_of(e0_d, q, u).rearrange(
                            "c (a n) -> c a n", a=2)).then_inc(e0_in[u // 2], 16)

                skewed(sp, [(2, load_x), (5, load_e0)])

                done(sp, q_done, b, 0, 0)

                def stage_q(q, u):
                    if isinstance(q, int) and 4 * q + u == 1:
                        all_done(sp, q_done, b)
                    if not (isinstance(q, int) and 4 * q + u < 2):
                        done(sp, read_made, b, q, u, 2)
                    sp.dma_start(four(flat(q_in(u))), chunk_rows(plane_a, chunk_of(q, u))).then_inc(q_staged[u % 2], 16)

                def store_x1(q, u):
                    done(sp, x1_done, b, q, u)
                    sp.dma_start(x1_d[chunk_of(q, u)], flat(x1_out(u))).then_inc(x1_stored[u % 2], 16)

                def save_x1_t(q, u):
                    done(sp, x1_t_done, b, q, u)
                    sp.dma_start(chunk_rows(plane_b, place_of(q, u)), four(flat(x1_t(u)))).then_inc(x1_t_saved[u % 2], 16)

                skewed(sp, [(0, stage_q), (4, store_x1), (6, save_x1_t)])

                begun = sp.snap(b * STEPS + (1 + CREDIT))
                whole = sp.snap(b * STEPS + (STEPS + CREDIT))
                convs_over = sp.snap(b * PAIRS + (PAIRS + CREDIT))
                following = sp.snap((b + 1) % B)
                all_moved(sp, x1_stored, b)
                sp.wait_ge(cols_made, begun)

                def load_x1(q, u):
                    if not (isinstance(q, int) and 4 * q + u < 4):
                        done(sp, v_made, b, q, u, 4)
                    sp.dma_start(flat(x1_in(u)), x1_d[q * UNROLL + u]).then_inc(x1_loaded[u % 4], 16)

                def reload_x1(q, u):
                    if not (isinstance(q, int) and 4 * q + u < 2):
                        done(sp, base_done, b, q, u, 2)
                    sp.dma_start(flat(x1_again(u)), x1_d[q * UNROLL + u]).then_inc(x1_reloaded[u % 2], 16)

                def stage_y(q, u):
                    if isinstance(q, int) and 4 * q + u < 2:
                        sp.wait_ge(back_done, whole)
                    else:
                        done(sp, outf_turned, b, q, u, 2)
                    sp.dma_start(four(flat(y_in(u))), rows_of(plane_b, q, u)).then_inc(y_staged[u % 2], 16)

                def load_next_x():
                    load_x_first(following)

                def load_next_e0():
                    sp.wait_ge(conv1, convs_over)
                    load_e0_first()

                def store_y(q, u):
                    done(sp, y_done, b, q, u)
                    if isinstance(q, int) and 4 * q + u == 0:
                        sp.nop(nofuse=True)
                    sp.dma_start(image_rows(out, b, q, u), flat(y_out(u))).then_inc(y_stored[u % 4], 16)

                skewed(sp, [(0, load_x1), (4, stage_y), (6, reload_x1), (1, at_end(load_next_x)),
                            (10, store_y), (4, at_end(load_next_e0))])
            all_moved(sp, y_stored, B - 1)
            for s in x_in + e0_in:
                sp.wait_ge(s, (B * (PAIRS // 2) + 2) * 16)

        @block.tensor
        def _(pe):
            mm = nc.tensor.matmul
            credit(pe, [e0_made, centered, normed, k_made, q_made, ctx_added, read_made, turned, projected,
                        x1_turned, gram_added, ff1_made, s_made, cols_made, rows_made, back_made, v_made,
                        outf_turned, outf_made, out_s_made, gate_f_made])
            pe.wait_ge(loads, 16 * n_setup)
            for i in range(len(WEIGHTS)):
                last = nc.tensor.transpose(bank[:, i // 4, (i % 4) * 128:(i % 4 + 1) * 128], nat[:, i, :], square("ident"))
            last.then_inc(pe_ready, 1)
            pe.wait_ge(dve_ready, 3)
            nc.tensor.transpose(bank[0:MAPS, 4, 0:128], tap_maps_w[:, :], square("ident")).then_inc(pe_ready, 1)
            mm(bank[:, 5, 0:1], head_of[:, :], scale8[:, :], start=True, stop=True).then_inc(pe_ready, 1)
            mm(bank[:, 7, 0:128], ctx_x[:, :], weight("v0"), start=True, stop=True)
            mm(bank[:, 6, 0:128], nat[:, WEIGHTS.index("proj_f"), :], weight("gate_fs"),
               start=True, stop=True).then_inc(pe_ready, 1)
            pe.wait_ge(dve_ready, 4)

            def make_e0(q, u):
                done(pe, e0_copied, 0, q, u, 2)
                mm(bank[:, u % 2, :], tap_maps_t[:, :], maps[:, bass.ds(q * (UNROLL * CHUNK) + u * CHUNK, CHUNK)],
                   start=True, stop=True).then_inc(e0_made, 1)

            for q in range(QUADS):
                pe.wait_ge(maps_in[q], 16)
                for u in range(UNROLL):
                    make_e0(q, u)

            with pe.Fori(0, B) as b:
                def center(q, u):
                    pair_done(pe, conv0, b, q, u)
                    done(pe, normed_t, b, q, u, 2)
                    for k in range(4):
                        last = mm(bank[:, u % 2, k * 128:(k + 1) * 128], flat(part(u))[:, k * 128:(k + 1) * 128],
                                  square("center"), start=True, stop=True)
                    last.then_inc(centered, 1)

                def turn_normed(q, u):
                    done(pe, normed_t, b, q, u)
                    done(pe, scaled, b, q, u, 1)
                    for k in range(4):
                        last = nc.tensor.transpose(bank[:, 2, k * 128:(k + 1) * 128], xhat[:, u, k, 0:128], square("ident"))
                    last.then_inc(normed, 1)

                def make_k(q, u):
                    done(pe, scaled, b, q, u)
                    done(pe, k_done, b, q, u, 2)
                    for k in range(4):
                        last = mm(bank[:, 3 + u % 2, k * 128:(k + 1) * 128], flat(xf(u))[:, k * 128:(k + 1) * 128],
                                  weight("k0"), start=True, stop=True)
                    last.then_inc(k_made, 1)

                def make_q(q, u):
                    done(pe, q_done, b, q, u, 1)
                    mm(bank[:, 5, :], weight("q0"), flat(xf(u)), start=True, stop=True).then_inc(q_made, 1)

                def add_context(q, u):
                    done(pe, k_done, b, q, u)
                    for k in range(4):
                        last = mm(bank[:, 6, 0:129], blocks(k_t(u))[:, k, :], xhat[:, u, k, :],
                                  start=False, stop=False)
                    last.then_inc(ctx_added, 1)

                pe.wait_ge(gate_f_done, b * STEPS + CREDIT)
                pe.wait_ge(gated, b * STEPS + CREDIT)
                mm(bank[:, 6, 0:129], zeros[:, 0:128], zeros[:, 0:129], start=True, stop=False)
                skewed(pe, [(2, turn_normed), (3, make_k), (3, make_q), (0, center), (4, add_context)])
                mm(bank[:, 6, 0:129], zeros[:, 0:128], zeros[:, 0:129], start=False, stop=True).then_inc(small_pe, 1)
                pe.wait_ge(small_dve, b * 10 + 1)
                nc.tensor.transpose(bank[:, 6, 0:128], ctx_x[:, :], square("ident")).then_inc(small_pe, 1)
                pe.wait_ge(small_dve, b * 10 + 2)
                mm(bank[:, 6, 0:128], ctx_t[:, :], weight("v0"), start=True, stop=True).then_inc(small_pe, 1)

                all_done(pe, q_done, b)
                pe.wait_ge(small_dve, b * 10 + 3)

                def read_out(q, u):
                    moved(pe, q_staged, b, q, u)
                    done(pe, divided, b, q, u, 1)
                    for k in range(4):
                        last = mm(bank[:, k // 2, (k % 2) * 256:(k % 2) * 256 + 136],
                                  flat(q_in(u))[:, k * 128:(k + 1) * 128], read[:, :], start=True, stop=True)
                    last.then_inc(read_made, 1)

                def turn_out(q, u):
                    done(pe, divided, b, q, u)
                    done(pe, out_done, b, q, u, 1)
                    for k in range(4):
                        last = nc.tensor.transpose(bank[:, 2, k * 128:(k + 1) * 128],
                                                   flat(out_t(u))[:, k * 128:(k + 1) * 128], square("ident"))
                    last.then_inc(turned, 1)

                def project(q, u):
                    done(pe, out_done, b, q, u)
                    done(pe, x1_done, b, q, u, 1)
                    mm(bank[:, 3, :], weight("proj0"), flat(out_c(u)), start=True, stop=True).then_inc(projected, 1)

                def turn_x1(q, u):
                    done(pe, x1_done, b, q, u)
                    done(pe, x1_t_done, b, q, u, 1)
                    for k in range(4):
                        to = in_place(u, k)
                        last = nc.tensor.transpose(bank[:, 4, to * 128:(to + 1) * 128],
                                                   flat(x1_out(u))[:, k * 128:(k + 1) * 128], square("ident"))
                    last.then_inc(x1_turned, 1)

                def make_ff1(q, u):
                    done(pe, gelu_done, b, q, u, 1)
                    mm(bank[:, 5, :], weight("ff1"), flat(x1_out(u)), start=True, stop=True).then_inc(ff1_made, 1)

                def add_gram(q, u):
                    done(pe, x1_t_done, b, q, u)
                    for k in range(4):
                        y = flat(x1_t(u))[:, k * 128:(k + 1) * 128]
                        last = mm(bank[:, 7, 0:128], y, y, start=False, stop=False)
                    last.then_inc(gram_added, 1)

                def make_s(q, u):
                    done(pe, gelu_done, b, q, u)
                    done(pe, s_done, b, q, u, 1)
                    for k in range(4):
                        to = in_place(u, k)
                        last = mm(bank[:, 6, to * 128:(to + 1) * 128], flat(gelu(u))[:, k * 128:(k + 1) * 128],
                                  weight("ff2"), start=True, stop=True)
                    last.then_inc(s_made, 1)

                mm(bank[:, 7, 0:128], zeros[:, 0:128], zeros[:, 0:128], start=True, stop=False)
                skewed(pe, [(0, read_out), (1, turn_out), (2, project), (3, turn_x1), (3, make_ff1),
                            (4, add_gram), (4, make_s)])
                mm(bank[:, 7, 0:128], zeros[:, 0:128], zeros[:, 0:128], start=False, stop=True).then_inc(small_pe, 1)
                all_done(pe, s_done, b)

                def columns(q, u):
                    for i, (slot, folded, split) in enumerate(((fold_x(u), folded_x, split_x), (fold_s(u), folded_s, split_s))):
                        done(pe, folded, b, q, u)
                        done(pe, split, b, q, u, 1)
                        for k in range(4):
                            last = mm(bank[:, i, k * 128:(k + 1) * 128], flat(slot)[:, k * 128:(k + 1) * 128],
                                      square("col_fwd"), start=True, stop=True)
                    last.then_inc(cols_made, 1)

                def rows(q, u):
                    done(pe, split_x, b, q, u)
                    done(pe, split_s, b, q, u)
                    done(pe, products, b, q, u, 1)
                    for i, (slot, m) in enumerate(((t1x(u), "row_even"), (t2x(u), "row_mix"),
                                                   (t1s(u), "row_even"), (t2s(u), "row_mix"))):
                        last = mm(bank[:, 2 + i, 0:4 * KW], square(m), ring[:, slot, 0:4 * KW], start=True, stop=True)
                    last.then_inc(rows_made, 1)

                def rows_back(q, u):
                    done(pe, packed, b, q, u)
                    done(pe, back_done, b, q, u, 1)
                    for k in range(4):
                        o = bank[:, 6, k * 128:(k + 1) * 128]
                        mm(o, flat(left(u, 0))[:, k * 128:(k + 1) * 128], square("row_cos"), start=True, stop=False)
                        last = mm(o, flat(left(u, 1))[:, k * 128:(k + 1) * 128], square("row_sin"),
                                  start=False, stop=True)
                    last.then_inc(back_made, 1)

                def score(q, u):
                    if isinstance(q, int) and 4 * q + u == 1:
                        pe.wait_ge(small_dve, b * 10 + 4)
                        mm(bank[:, 7, 0:128], gram[:, :], weight("k1"), start=True, stop=True).then_inc(small_pe, 1)
                    if isinstance(q, int) and 4 * q + u == 2:
                        pe.wait_ge(small_dve, b * 10 + 5)
                        mm(bank[:, 7, 0:128], weight("q1"), gram_k[:, :], start=True, stop=True).then_inc(small_pe, 1)

                def make_v(q, u):
                    moved(pe, x1_loaded, b, q, u)
                    done(pe, v_saved, b, q, u, 1)
                    mm(bank[:, 0, :], weight("v1"), flat(x1_in(u)), start=True, stop=True).then_inc(v_made, 1)

                def make_mix():
                    pe.wait_ge(small_dve, b * 10 + 9)
                    mm(bank[:, 7, 0:128], attn[:, :], weight("proj_s"), start=True, stop=True).then_inc(small_pe, 1)

                def make_first_v():
                    all_done(pe, split_x, b)
                    make_v(0, 0)

                skewed(pe, [(0, columns), (0, score), (1, at_end(make_first_v)), (1, rows),
                            (1, at_end(lambda: make_v(0, 1), make_mix)), (2, at_end(lambda: make_v(0, 2))), (3, rows_back)])

                def columns_back(q, u):
                    moved(pe, y_staged, b, q, u)
                    done(pe, outf_copied, b, q, u, 1)
                    for k in range(4):
                        last = mm(bank[:, 1, k * 128:(k + 1) * 128], flat(y_in(u))[:, k * 128:(k + 1) * 128],
                                  square("col_inv"), start=True, stop=True)
                    last.then_inc(outf_turned, 1)

                def project_f(q, u):
                    done(pe, outf_copied, b, q, u)
                    done(pe, gated, b, q, u, 2)
                    done(pe, gate_s_done, b, q, u, 1)
                    mm(bank[:, 2 + u % 2, :], weight("proj_f"), flat(outf_in(u)), start=True, stop=True)
                    mm(bank[:, 4, :], weight("gate_fs"), flat(outf_in(u)), start=True, stop=True).then_inc(outf_made, 1)

                def project_s(q, u):
                    if isinstance(q, int) and 4 * q + u == 0:
                        pe.wait_ge(small_dve, b * 10 + 10)
                    pair_done(pe, conv1, b, q, u)
                    done(pe, out_s_done, b, q, u, 1)
                    mm(four(bank[:, 5, :]), mix[:, :], rows_of(plane_a, q, u), start=True, stop=False)
                    mm(bank[:, 5, :], weight("proj_s"), flat(conv_v(u)), start=False, stop=True).then_inc(out_s_made, 1)

                def make_gate_f(q, u):
                    done(pe, out_s_done, b, q, u)
                    done(pe, gate_f_done, b, q, u, 1)
                    mm(bank[:, 6, :], weight("gate_sf"), flat(out_s(u)), start=True, stop=True).then_inc(gate_f_made, 1)

                skewed(pe, [(0, after(3, make_v)), (5, columns_back), (6, make_gate_f), (6, project_f), (5, project_s)])

        @block.scalar
        def _(act):
            op = nc.scalar.activation
            credit(act, [last_taps, last_taps_v, e0_copied, squared, scaled, k_done, q_done, out_done, x1_t_done,
                         gelu_done, split_x, spec_done, back_done, v_saved, outf_copied, gate_s_done, out_s_done, gate_f_done])

            def copy_e0(q, u):
                done(act, e0_made, 0, q, u)
                moved(act, e0_out, 0, q, u, 4)
                op(flat(part(u)), bank[:, u % 2, :], ACT.Copy).then_inc(e0_copied, 1)

            for q in range(QUADS):
                for u in range(UNROLL):
                    copy_e0(q, u)
            act.wait_ge(dve_ready, 7)

            def make_last_taps(b, q, u):
                if u % 2 == 0:
                    pair_moved(act, x_in, b, q, u)
                done(act, seeded, b, q, u, 4)
                for i, t in enumerate(range(DVE_TAPS[0], TAPS)):
                    last = op(four(flat(tap(u, i))), tap_rows(plane_b, q, u, t), ACT.Copy, scale=taps0[:, t:t + 1])
                last.then_inc(last_taps, 1)

            for u in range(2):
                make_last_taps(0, 0, u)

            with act.Fori(0, B) as b:
                act.wait_ge(base_done, b * STEPS + CREDIT)

                def square_up(q, u):
                    done(act, centered, b, q, u)
                    done(act, normed_t, b, q, u, 2)
                    for k in range(4):
                        last = op(ring[:, junk, k * 128:(k + 1) * 128], bank[:, u % 2, k * 128:(k + 1) * 128],
                                  ACT.Square, accum_out=sumsq[:, u % 2, k:k + 1])
                    last.then_inc(ln_chain, 1)
                    act.wait_ge(ln_chain, b * STEPS + q * UNROLL + (u + 1))
                    op(std[:, u % 2, :], sumsq[:, u % 2, :], ACT.Sqrt, bias=eps[:, :], scale=1.0 / C).then_inc(squared, 1)

                def scale_shift(q, u):
                    done(act, normed, b, q, u)
                    done(act, k_made, b, q, u, 2)
                    done(act, q_made, b, q, u, 2)
                    op(flat(xf(u)), bank[:, 2, :], ACT.Identity, bias=vector("ln_b"), scale=vector("ln_g")).then_inc(scaled, 1)

                def finish_k(q, u):
                    done(act, k_made, b, q, u)
                    done(act, ctx_added, b, q, u, 2)
                    op(flat(k_t(u)), bank[:, 3 + u % 2, :], ACT.Relu).then_inc(k_done, 1)

                def finish_q(q, u):
                    done(act, q_made, b, q, u)
                    op(rows_of(plane_a, q, u), four(bank[:, 5, :]), ACT.Relu).then_inc(q_done, 1)

                skewed(act, [(9, scale_shift), (10, finish_k), (7, square_up), (10, finish_q),
                             (2, after(2, lambda q, u: make_last_taps(b, q, u)))])

                def copy_out(q, u):
                    done(act, turned, b, q, u)
                    done(act, projected, b, q, u, 2)
                    op(flat(out_c(u)), bank[:, 2, :], ACT.Copy).then_inc(out_done, 1)

                def copy_x1_t(q, u):
                    done(act, x1_turned, b, q, u)
                    done(act, gram_added, b, q, u, 2)
                    moved(act, x1_t_saved, b, q, u, 2)
                    op(flat(x1_t(u)), bank[:, 4, :], ACT.Copy).then_inc(x1_t_done, 1)

                def make_gelu(q, u):
                    done(act, ff1_made, b, q, u)
                    done(act, s_made, b, q, u, 2)
                    op(flat(gelu(u)), bank[:, 5, :], ACT.Gelu).then_inc(gelu_done, 1)

                skewed(act, [(1, copy_out), (3, copy_x1_t), (3, make_gelu)])

                def exponents(q, u):
                    if isinstance(q, int) and 4 * q + u == 3:
                        act.wait_ge(small_dve, b * 10 + 7)
                        op(probs[:, :], scores[:, :], ACT.Exp, bias=peak[:, :], accum_out=total[:, :]).then_inc(small_act, 1)

                def split(q, u):
                    done(act, cols_made, b, q, u)
                    done(act, rows_made, b, q, u, 2)
                    cols = bank[:, 0, :].rearrange("p (k n) -> p k n", n=128)
                    re, im = slice(0, KW), slice(KW, 128)
                    one, two = blocks(t1x(u), KW), blocks(t2x(u), KW)
                    op(one[0:HALF, :, :], cols[0:HALF, :, re], ACT.Copy)
                    op(one[HALF:128, :, 1:KW - 1], cols[HALF:128, :, im], ACT.Copy)
                    op(two[0:HALF, :, 1:KW - 1], cols[0:HALF, :, im], ACT.Copy)
                    op(two[HALF:128, :, :], cols[HALF:128, :, re], ACT.Copy).then_inc(split_x, 1)

                def copy_spec(q, u):
                    done(act, rows_made, b, q, u)
                    done(act, products, b, q, u, 1)
                    op(ring[:, spec_x(0), 0:4 * KW], bank[:, 2, 0:4 * KW], ACT.Copy)
                    op(ring[:, spec_x(1), 0:4 * KW], bank[:, 3, 0:4 * KW], ACT.Copy).then_inc(spec_done, 1)

                def copy_back(q, u):
                    done(act, back_made, b, q, u)
                    group = plane_b[:, 1:H + 1, bass.ds(q * (UNROLL * GROUP) + (u * GROUP + 1), GROUP)]
                    op(group.rearrange("p h c -> p c h"), bank[:, 6, :].rearrange("p (k n) -> p k n", n=128),
                       ACT.Copy).then_inc(back_done, 1)

                def save_v(q, u):
                    done(act, v_made, b, q, u)
                    op(rows_of(plane_a, q, u), four(bank[:, 0, :]), ACT.Copy).then_inc(v_saved, 1)

                def make_last_taps_v(q, u):
                    if isinstance(q, int) and 4 * q + u == STEPS - 1:
                        done(act, v_saved, b, q, u)
                    else:
                        done(act, v_saved, b, q, u, -1)
                    pair_done(act, conv1, b, q, u, 2)
                    done(act, seeded_v, b, q, u, 2)
                    op(four(flat(seed_v(u))), tap_rows(plane_a, q, u, TAPS - 2), ACT.Copy, scale=taps1[:, TAPS - 2:TAPS - 1])
                    op(four(flat(tap_v(u))), tap_rows(plane_a, q, u, TAPS - 1), ACT.Copy,
                       scale=taps1[:, TAPS - 1:TAPS]).then_inc(last_taps_v, 1)

                skewed(act, [(0, exponents), (0, split), (1, at_end(lambda: save_v(0, 0))), (1, copy_spec),
                             (1, at_end(lambda: save_v(0, 1), lambda: make_last_taps_v(0, 0))),
                             (2, at_end(lambda: save_v(0, 2), lambda: make_last_taps_v(0, 1))), (3, copy_back)])

                def copy_outf(q, u):
                    done(act, outf_turned, b, q, u)
                    done(act, outf_made, b, q, u, 2)
                    op(flat(outf_in(u)), bank[:, 1, :], ACT.Copy).then_inc(outf_copied, 1)

                def finish_gate_s(q, u):
                    done(act, outf_made, b, q, u)
                    done(act, base_done, b, q, u, 2)
                    op(flat(gate_s(u)), bank[:, 4, :], ACT.Sigmoid, bias=vector("b_gfs")).then_inc(gate_s_done, 1)

                def copy_out_s(q, u):
                    done(act, out_s_made, b, q, u)
                    done(act, gate_f_made, b, q, u, 2)
                    done(act, base_done, b, q, u, 2)
                    op(flat(out_s(u)), bank[:, 5, :], ACT.Copy).then_inc(out_s_done, 1)

                def finish_gate_f(q, u):
                    done(act, gate_f_made, b, q, u)
                    done(act, gated, b, q, u, 2)
                    op(flat(gate_f(u)), bank[:, 6, :], ACT.Sigmoid, bias=vector("b_gsf")).then_inc(gate_f_done, 1)

                skewed(act, [(0, after(3, save_v)), (1, after(2, make_last_taps_v)), (5, copy_outf), (6, finish_gate_f),
                             (6, finish_gate_s), (5, copy_out_s),
                             (4, at_end(lambda: all_done(act, seeded_v, b), lambda: make_last_taps(b + 1, 0, 0))),
                             (5, at_end(lambda: make_last_taps(b + 1, 0, 1)))])

        def fold(eng, plane, o, q, u):
            c = bass.ds(q * (UNROLL * GROUP) + (u * GROUP + 1), GROUP)
            low = plane[:, 1:HALF + 1, c].rearrange("p h c -> p c h")
            high = plane[:, HALF + 1:H + 1, c].rearrange("p h c -> p c h")
            eng.tensor_tensor(o[:, :, 0:HALF], low, high, ALU.add)
            return eng.tensor_tensor(o[:, :, HALF:128], low, high, ALU.subtract)

        @block.vector
        def _(dve):
            v = nc.vector
            credit(dve, [folded_x, conv0, normed_t, divided, x1_done, s_done, folded_s, split_s, products, conv1, gated, y_done])
            v.memset(zeros[:, :], 0.0)
            v.memset(eps[:, :], LN_EPS)
            v.memset(xhat[:, :, :, 128:129], 1.0)
            dve.wait_ge(loads, 16 * n_setup)
            v.tensor_copy(ctx_x[:, :], vector("ln_b").broadcast_to([128, 128]))
            for p in range(2):
                v.tensor_scalar(tap_maps_w[:, 0:2 * TAPS].rearrange("p (t e) -> p t e", e=2)[:, :, p], taps0[:, :],
                                parity[:, p:p + 1], None, ALU.mult)
            v.tensor_copy(tap_maps_w[:, 2 * TAPS:MAPS], vector("conv_b")).then_inc(dve_ready, 1)
            dve.wait_ge(pe_ready, 1)
            v.tensor_copy(weights[:, 0:8, :], bank[:, 0:2, :].rearrange("p a (k n) -> p (a k) n", n=128)).then_inc(dve_ready, 1)
            v.tensor_copy(weights[:, 8:13, :], bank[:, 2:4, :].rearrange("p a (k n) -> p (a k) n", n=128)[:, 0:5, :]
                          ).then_inc(dve_ready, 1)
            dve.wait_ge(pe_ready, 4)
            v.tensor_copy(tap_maps_t[:, :], bank[0:MAPS, 4, 0:128]).then_inc(dve_ready, 1)
            v.tensor_copy(scale_col[:, :], bank[:, 5, 0:1])
            v.tensor_copy(shift_v[:, :], bank[:, 7, 0:128])
            v.tensor_scalar(weight("v0"), weight("v0"), vector("ln_g"), None, ALU.mult)
            v.tensor_copy(weight("gate_fs"), bank[:, 6, 0:128]).then_inc(dve_ready, 1)
            for plane in (plane_b, plane_a):
                if plane is plane_a:
                    all_done(dve, e0_copied, 0)
                v.memset(plane[:, 0, :], 0.0)
                v.memset(plane[:, H + 1, :], 0.0)
                v.memset(plane[:, 1:H + 1, 0:1], 0.0)
                v.memset(plane[:, 1:H + 1, W + 1:W + 2], 0.0).then_inc(dve_ready, 1)

            def half_of(layer, w):
                n = DVE_TAPS[layer]
                return range((n + 1) // 2, n) if w % 2 else range((n + 1) // 2)

            def conv(layer, plane, taps, slots, seeds, b, q, w, finished, some):
                n = DVE_TAPS[layer]
                counts = [2 * k - 1 for k in DVE_TAPS]
                seen = (b * (PAIRS * sum(counts)) + q * (UNROLL // 2 * counts[layer])
                        + (w // 2 * counts[layer] + layer * PAIRS * counts[0]))
                for t in some:
                    for i in range(2):
                        o = four(flat(slots[i]))
                        if t:
                            dve.wait_ge(dve_chain, seen + (2 * (t - 1) + i + 1))
                        ins = v.scalar_tensor_tensor(out=o, in0=plane(i, t), scalar=taps[:, t:t + 1],
                                                     in1=o if t else four(flat(seeds[i])), op0=ALU.mult, op1=ALU.add)
                        ins.then_inc(finished if t == n - 1 and i else dve_chain, 1)

            with dve.Fori(0, B) as b:
                for s in y_stored:
                    dve.wait_ge(s, b * (STEPS // 4 * 16) + 16)

                def conv_x(q, w):
                    u = w // 2 * 2
                    if w == u:
                        done(dve, seeded, b, q, u, -1)
                        done(dve, centered, b, q, u, 3)
                    conv(0, lambda i, t: tap_rows(plane_b, q, u + i, t), taps0, (part(u), part(u + 1)),
                         (seeds(u), seeds(u + 1)), b, q, w, conv0, half_of(0, w)[:-1])

                def conv_x_on(q, w):
                    u = w // 2 * 2
                    conv(0, lambda i, t: tap_rows(plane_b, q, u + i, t), taps0, (part(u), part(u + 1)),
                         (seeds(u), seeds(u + 1)), b, q, w, conv0, half_of(0, w)[-1:])

                def invert(q, u):
                    done(dve, squared, b, q, u)
                    done(dve, normed_t, b, q, u, 2)
                    v.reciprocal(rstd[:, u % 2, :], std[:, u % 2, :]).then_inc(small_chain, 1)

                def normalize(q, u):
                    dve.wait_ge(small_chain, b * (3 * STEPS) + q * UNROLL + (u + 1))
                    done(dve, ctx_added, b, q, u, 4)
                    v.tensor_tensor(xhat[:, u, :, 0:128], bank[:, u % 2, :].rearrange("p (k n) -> p k n", n=128),
                                    rstd[:, u % 2, :].unsqueeze(2).broadcast_to([128, 4, 128]), ALU.mult).then_inc(normed_t, 1)

                skewed(dve, [(0, conv_x), (2, invert), (0, conv_x_on), (2, normalize)])
                dve.wait_ge(small_pe, b * 7 + 1)
                v.tensor_copy(ksum[:, :], bank[:, 6, 128:129]).then_inc(ksum_done, 1)
                v.tensor_copy(ctx_x[:, :], bank[:, 6, 0:128]).then_inc(small_dve, 1)
                dve.wait_ge(small_pe, b * 7 + 2)
                v.tensor_copy(ctx_t[:, :], bank[:, 6, 0:128]).then_inc(small_dve, 1)
                dve.wait_ge(ksum_done, b * 2 + 1)
                v.tensor_scalar(read[:, 128:136], head_cols, ksum[:, :], None, ALU.mult)
                dve.wait_ge(small_pe, b * 7 + 3)
                v.scalar_tensor_tensor(out=ctx_x[:, :], in0=shift_v[:, :], scalar=ksum[:, :], in1=bank[:, 6, 0:128],
                                       op0=ALU.mult, op1=ALU.add).then_inc(ksum_done, 1)
                dve.wait_ge(ksum_done, b * 2 + 2)
                v.tensor_tensor(read[:, 0:128], ctx_x[:, :], square("head_mask"), ALU.mult).then_inc(small_dve, 1)

                def divide(q, u):
                    done(dve, read_made, b, q, u)
                    n = bank[:, 0:2, :].rearrange("p a (k n) -> p (a k) n", n=256)
                    d = den[:, u % 2, :].rearrange("p (k h) -> p k h", h=HEADS)
                    v.tensor_scalar(d, n[:, :, 128:136], DEN_MIN, None, ALU.max).then_inc(small_chain, 1)
                    dve.wait_ge(small_chain, b * (3 * STEPS) + q * (2 * UNROLL) + (STEPS + 2 * u + 1))
                    v.reciprocal(rden[:, u % 2, :], den[:, u % 2, :]).then_inc(small_chain, 1)
                    dve.wait_ge(small_chain, b * (3 * STEPS) + q * (2 * UNROLL) + (STEPS + 2 * u + 2))
                    done(dve, turned, b, q, u, 2)
                    r = rden[:, u % 2, :].rearrange("p (k h) -> p k h", h=HEADS)
                    v.tensor_tensor(blocks(out_t(u)).rearrange("p k (h d) -> p k h d", d=HEAD),
                                    n[:, :, 0:128].rearrange("p k (h d) -> p k h d", d=HEAD),
                                    r.unsqueeze(3).broadcast_to([128, 4, HEADS, HEAD]), ALU.mult).then_inc(divided, 1)

                def add_x(q, u):
                    done(dve, projected, b, q, u)
                    done(dve, ff1_made, b, q, u, 2)
                    done(dve, x1_turned, b, q, u, 2)
                    moved(dve, x1_stored, b, q, u, 2)
                    v.scalar_tensor_tensor(out=four(flat(x1_out(u))), in0=four(bank[:, 3, :]), scalar=vector("proj_b"),
                                           in1=chunk_rows(plane_b, chunk_of(q, u)), op0=ALU.add, op1=ALU.add).then_inc(x1_done, 1)

                def save_s(q, u):
                    done(dve, s_made, b, q, u)
                    if u == 1:
                        moved(dve, q_staged, b, q, u, -2)
                    v.tensor_copy(chunk_rows(plane_a, place_of(q, u)), four(bank[:, 6, :])).then_inc(s_done, 1)

                def clear_edges(q, u):
                    if not (isinstance(q, int) and 4 * q + u == 3):
                        return
                    for k in range(2):
                        for one, two in ((t1x(k), t2x(k)), (t1s(k), t2s(k))):
                            v.memset(blocks(one, KW)[HALF:128, :, 0:KW:KW - 1], 0.0)
                            v.memset(blocks(two, KW)[0:HALF, :, 0:KW:KW - 1], 0.0)

                skewed(dve, [(0, divide), (0, clear_edges), (2, add_x), (4, save_s)])

                all_done(dve, s_done, b)
                all_done(dve, gram_added, b)
                all_done(dve, s_made, b)
                all_moved(dve, x1_t_saved, b)
                all_moved(dve, x1_stored, b)

                def softmax(q, u):
                    if not (isinstance(q, int) and q == 0):
                        return
                    if u == 0:
                        dve.wait_ge(small_pe, b * 7 + 4)
                        v.tensor_copy(gram[:, :], bank[:, 7, 0:128]).then_inc(small_dve, 1)
                    if u == 1:
                        dve.wait_ge(small_pe, b * 7 + 5)
                        v.tensor_copy(gram_k[:, :], bank[:, 7, 0:128]).then_inc(small_dve, 1)
                    if u == 2:
                        dve.wait_ge(small_pe, b * 7 + 6)
                        v.scalar_tensor_tensor(out=scores[:, :], in0=bank[:, 7, 0:128], scalar=scale_col[:, :],
                                               in1=square("head_off"), op0=ALU.mult, op1=ALU.add).then_inc(small_dve, 1)
                        dve.wait_ge(small_dve, b * 10 + 6)
                        v.tensor_reduce(peak[:, :], scores[:, :], mybir.AxisListType.X, ALU.max,
                                        negate=True).then_inc(small_dve, 1)
                    if u == 3:
                        dve.wait_ge(small_act, b + 1)
                        v.reciprocal(rtotal[:, :], total[:, :]).then_inc(small_dve, 1)
                        dve.wait_ge(small_dve, b * 10 + 8)
                        v.tensor_scalar(attn[:, :], probs[:, :], rtotal[:, :], None, ALU.mult).then_inc(small_dve, 1)

                def fold_up(q, u):
                    done(dve, cols_made, b, q, u, 2)
                    fold(v, plane_b, blocks(fold_x(u)), q, u).then_inc(folded_x, 1)
                    fold(v, plane_a, blocks(fold_s(u)), q, u).then_inc(folded_s, 1)

                def split_up_s(q, u):
                    done(dve, cols_made, b, q, u)
                    done(dve, rows_made, b, q, u, 2)
                    cols = bank[:, 1, :].rearrange("p (k n) -> p k n", n=128)
                    re, im = slice(0, KW), slice(KW, 128)
                    one, two = blocks(t1s(u), KW), blocks(t2s(u), KW)
                    v.tensor_copy(one[0:HALF, :, :], cols[0:HALF, :, re])
                    v.tensor_copy(one[HALF:128, :, 1:KW - 1], cols[HALF:128, :, im])
                    v.tensor_copy(two[0:HALF, :, 1:KW - 1], cols[0:HALF, :, im])
                    v.tensor_copy(two[HALF:128, :, :], cols[HALF:128, :, re]).then_inc(split_s, 1)

                def multiply(q, u):
                    done(dve, spec_done, b, q, u)
                    done(dve, packed, b, q, u, 2)
                    for i, (xs, ss) in enumerate(((0, 4), (1, 5), (0, 5), (1, 4))):
                        last = v.tensor_tensor(ring[:, prod(u, i), 0:4 * KW], ring[:, spec_x(xs), 0:4 * KW],
                                               bank[:, ss, 0:4 * KW], ALU.mult)
                    last.then_inc(products, 1)

                skewed(dve, [(0, fold_up), (1, split_up_s), (2, multiply), (0, softmax)])

                dve.wait_ge(small_pe, b * 7 + 7)
                v.tensor_copy(mix[:, :], bank[:, 7, 0:128]).then_inc(small_dve, 1)
                all_done(dve, products, b)

                def conv_of_v(q, w):
                    u = w // 2 * 2
                    if w == u:
                        done(dve, seeded_v, b, q, u, -1)
                        done(dve, out_s_made, b, q, u, 3)
                    conv(1, lambda i, t: tap_rows(plane_a, q, u + i, t), taps1, (conv_v(u), conv_v(u + 1)),
                         (seed_v(u), seed_v(u + 1)), b, q, w, conv1, half_of(1, w))

                def gate_out_f(q, u):
                    done(dve, gate_f_done, b, q, u)
                    done(dve, outf_made, b, q, u)
                    moved(dve, y_stored, b, q, u, 4)
                    v.tensor_tensor(flat(y_out(u)), bank[:, 2 + u % 2, :], flat(gate_f(u)), ALU.mult).then_inc(gated, 1)

                def finish(q, u):
                    done(dve, gated, b, q, u)
                    done(dve, base_done, b, q, u)
                    v.tensor_tensor(flat(y_out(u)), flat(y_out(u)), flat(base(u)), ALU.add).then_inc(y_done, 1)

                skewed(dve, [(3, conv_of_v), (7, gate_out_f), (7, finish)])

        @block.gpsimd
        def _(pool):
            g = nc.gpsimd
            credit(pool, [seeded, seeded_v, packed, base_done])
            def seed(b, q, u):
                done(pool, last_taps, b, q, u)
                pair_moved(pool, e0_in, b, q, u)
                pair_done(pool, conv0, b, q, u, 2)
                to = flat(seeds(u))
                g.tensor_tensor(to, flat(e0(u)), flat(tap(u, 0)), ALU.add).then_inc(seed_chain, 1)
                pool.wait_ge(seed_chain, b * (2 * STEPS) + q * (2 * UNROLL) + (2 * u + 1))
                g.tensor_tensor(to, to, flat(tap(u, 1)), ALU.add).then_inc(seed_chain, 1)
                pool.wait_ge(seed_chain, b * (2 * STEPS) + q * (2 * UNROLL) + (2 * u + 2))
                g.tensor_tensor(to, to, flat(tap(u, 2)), ALU.add).then_inc(seeded, 1)

            for u in range(2):
                seed(0, 0, u)

            with pool.Fori(0, B) as b:
                pool.wait_ge(base_done, b * STEPS + CREDIT)

                skewed(pool, [(1, after(2, lambda q, u: seed(b, q, u)))])

                def pack(q, u):
                    done(pool, products, b, q, u)
                    done(pool, back_made, b, q, u, 2)
                    rr, ii, ri, ir = (blocks(prod(u, i), KW) for i in range(4))
                    one, two = blocks(left(u, 0)), blocks(left(u, 1))
                    mid = slice(1, KW - 1)
                    g.tensor_tensor(one[:, :, 0:KW], rr, ii, ALU.subtract)
                    g.tensor_tensor(one[:, :, KW:128], ri[:, :, mid], ir[:, :, mid], ALU.add)
                    g.tensor_tensor(two[:, :, 0:KW], ri, ir, ALU.add)
                    g.tensor_tensor(two[:, :, KW:128], ii[:, :, mid], rr[:, :, mid], ALU.subtract).then_inc(packed, 1)

                skewed(pool, [(0, pack)])

                def gate_out_s(q, u):
                    done(pool, gate_s_done, b, q, u)
                    done(pool, out_s_done, b, q, u)
                    done(pool, y_done, b, q, u, 2)
                    g.tensor_tensor(flat(base(u)), flat(out_s(u)), flat(gate_s(u)), ALU.mult).then_inc(pool_chain, 1)
                    pool.wait_ge(pool_chain, b * STEPS + q * UNROLL + (u + 1))
                    moved(pool, x1_reloaded, b, q, u)
                    g.tensor_tensor(flat(base(u)), flat(base(u)), flat(x1_again(u)), ALU.add).then_inc(base_done, 1)

                def seed_of_v(q, u):
                    done(pool, last_taps_v, b, q, u)
                    g.tensor_tensor(flat(seed_v(u)), flat(seed_v(u)), flat(tap_v(u)), ALU.add).then_inc(seeded_v, 1)

                skewed(pool, [(1, seed_of_v), (6, gate_out_s), (4, at_end(lambda: seed(b + 1, 0, 0))),
                              (6, at_end(lambda: seed(b + 1, 0, 1)))])


_ARGS = {
    "proj_b": "L0_conv_proj_b", "conv_b": "L0_conv_conv_b", "ln_g": "L0_conv_ln_g", "ln_b": "L0_conv_ln_b",
    "b_gsf": "L1_conv_b_gsf", "b_gfs": "L1_conv_b_gfs", "scale_s": "L1_conv_scale_s",
    "conv_w": "L0_conv_conv_w", "W_dw": "L1_conv_W_dw", "proj0": "L0_conv_proj_w", "proj_s": "L1_conv_W_proj_s",
    "ff1": "L1_conv_W_ff1", "ff2": "L1_conv_W_ff2", "proj_f": "L1_conv_W_proj_f", "gate_sf": "L1_conv_W_gsf",
    "gate_fs": "L1_conv_W_gfs",
}


def kernel(**inputs):
    import concourse.bacc as bacc
    from concourse.bass_utils import run_bass_kernel_spmd

    nc = bacc.Bacc("TRN2", target_bir_lowering=False, num_devices=1, dynamic_dma_scratch_size=2048)
    arrays = {name: np.ascontiguousarray(a) for name, a in inputs.items()}
    arrays["x"] = arrays["x"].reshape(-1, C, PIX)
    arrays.update(shape_constants())
    aps = {name: nc.dram_tensor("in_" + name, a.shape, F32, kind="ExternalInput").ap() for name, a in arrays.items()}
    out = nc.dram_tensor("out", (B, C, PIX), F32, kind="ExternalOutput").ap()
    w = {short: aps[name] for short, name in _ARGS.items()}
    for i, part in enumerate("qkv"):
        w[f"{part}0"] = aps["L0_conv_qkv_w"][i * C:(i + 1) * C, :]
        w[f"{part}1"] = aps["L1_conv_W_qkv"][i * C:(i + 1) * C, :]
    conv_seq_kernel(nc, aps["x"], w, aps["squares"], aps["parity"], aps["head_of"], aps["head_cols"], aps["maps"], out)
    result = run_bass_kernel_spmd(nc, [{"in_" + name: a for name, a in arrays.items()}], core_ids=[0])
    return result.results[0]["out"].reshape(B, C, H, W)
```
